# Optimizing a Trainium2 kernel written in Bass

```python
import numpy as np
import jax
import jax.numpy as jnp

def _softmax(x, axis=-1):
    return jax.nn.softmax(x, axis=axis)

def _gelu(x):
    return jax.nn.gelu(x, approximate=True)

def _silu(x):
    return jax.nn.silu(x)

def _sigmoid(x):
    return jax.nn.sigmoid(x)

def _layernorm(x, axis=-1, eps=1e-05):
    m = jnp.mean(x, axis=axis, keepdims=True)
    v = jnp.var(x, axis=axis, keepdims=True)
    return (x - m) / jnp.sqrt(v + eps)

def _scatter_add(tgt, idx, src, axis=0):
    return tgt.at[idx].add(src)

def _segment_sum(src, seg, n):
    return jax.ops.segment_sum(src, seg, n)
kernel_name = 'mk_gnn_preln_d4_gnn_r8_49b0ad'

def setup_inputs(seed: int=0):
    np.random.seed(seed)
    _w = jnp.asarray

    def _rec_inputs():
        import jax
        import jax.numpy as jnp
        _gk = jax.random.key(seed)
        x = -0.000202 + 1 * jax.random.normal(jax.random.fold_in(_gk, 1), (6250, 128), jnp.float32)
        _s = jax.random.randint(jax.random.fold_in(_gk, 2), (100000,), 0, 6250, jnp.int32)
        _d = jax.random.randint(jax.random.fold_in(_gk, 3), (100000,), 0, 6250, jnp.int32)
        _loop = jnp.arange(6250, dtype=jnp.int32)
        src = jnp.concatenate([_s, _d, _loop])
        dst = jnp.concatenate([_d, _s, _loop])
        _o = jnp.argsort(dst, stable=True)
        src = src[_o]
        dst = dst[_o]
        edge_attr_3 = -0.000451519 + 1.00018 * jax.random.normal(jax.random.fold_in(_gk, 12), (206250, 3), jnp.float32)
        edge_weight = jax.random.uniform(jax.random.fold_in(_gk, 14), (206250,), jnp.float32, 0.0, 0.999998)
        return (x, src, dst, edge_attr_3, edge_weight)
    x, src, dst, edge_attr_3, edge_weight = _rec_inputs()

    def _L0_gnn_setup():
        import jax, jax.numpy as jnp
        import numpy as np
        N = 6250
        E = 200000
        IN = 128
        H = 4
        F = 32
        D = H * F
        key = jax.random.key(seed)
        ks = jax.random.split(key, 8)
        return {'x': jax.random.normal(ks[0], (N, IN), jnp.float32), 'src': jax.random.randint(ks[1], (E,), 0, N, jnp.int32), 'dst': jax.random.randint(ks[2], (E,), 0, N, jnp.int32), 'W': jax.random.normal(ks[3], (IN, D), jnp.float32) / np.sqrt(IN).astype(np.float32), 'attn_l': jax.random.normal(ks[4], (H, F), jnp.float32), 'attn_r': jax.random.normal(ks[5], (H, F), jnp.float32), 'bias': jnp.zeros((D,), jnp.float32), 'Wo': jax.random.normal(ks[6], (D, D), jnp.float32) / np.sqrt(D).astype(np.float32), 'bo': jnp.zeros((D,), jnp.float32), 'gamma': jnp.ones((D,), jnp.float32), 'beta': jnp.zeros((D,), jnp.float32)}
    _L0_gnn_all = _L0_gnn_setup()
    _L0_gnn_in = {k: v for k, v in _L0_gnn_all.items() if k in ('W', 'attn_l', 'attn_r', 'bias', 'Wo', 'bo', 'gamma', 'beta')}
    del _L0_gnn_all

    def _L1_gnn_setup():
        import jax, jax.numpy as jnp
        import numpy as np
        N_NODES = 6250
        N_EDGES = 100000
        IN_CH = 128
        OUT_CH = 128
        key = jax.random.key(seed)
        ks = jax.random.split(key, 8)
        x = jax.random.normal(ks[0], (N_NODES, IN_CH), dtype=jnp.float32)
        edge_index = jax.random.randint(ks[1], (2, N_EDGES), 0, N_NODES, dtype=jnp.int64)
        edge_weight = jax.random.uniform(ks[2], (N_EDGES,), dtype=jnp.float32)
        bound = 1.0 / np.sqrt(IN_CH)
        weight = jax.random.uniform(ks[3], (IN_CH, OUT_CH), minval=-bound, maxval=bound, dtype=jnp.float32)
        lin1_w = jax.random.uniform(ks[4], (OUT_CH, IN_CH), minval=-bound, maxval=bound, dtype=jnp.float32)
        lin1_b = jax.random.uniform(ks[5], (OUT_CH,), minval=-bound, maxval=bound, dtype=jnp.float32)
        lin2_w = jax.random.uniform(ks[6], (OUT_CH, IN_CH), minval=-bound, maxval=bound, dtype=jnp.float32)
        lin2_b = jax.random.uniform(ks[7], (OUT_CH,), minval=-bound, maxval=bound, dtype=jnp.float32)
        return {'x': x, 'edge_index': edge_index, 'edge_weight': edge_weight, 'weight': weight, 'lin1_w': lin1_w, 'lin1_b': lin1_b, 'lin2_w': lin2_w, 'lin2_b': lin2_b}
    _L1_gnn_all = _L1_gnn_setup()
    _L1_gnn_in = {k: v for k, v in _L1_gnn_all.items() if k in ('weight', 'lin1_w', 'lin1_b', 'lin2_w', 'lin2_b')}
    del _L1_gnn_all

    def _L2_gnn_setup():
        import jax, jax.numpy as jnp
        import numpy as np
        N = 6250
        E = 100000
        MUL = 32
        NB = 8
        R_MAX = 1.0
        AVG = 16.0
        SQ3 = 3.0 ** 0.5

        def _radial_embedding(r):
            x = jnp.clip(r / R_MAX, 0.0, 1.0)
            centers = jnp.arange(NB, dtype=jnp.float32) / (NB - 1)
            sigma = 1.0 / (NB - 1)
            emb = jnp.exp(-0.5 * ((x[:, None] - centers[None, :]) / sigma) ** 2)
            emb = emb * NB ** 0.5 * (r <= R_MAX).astype(jnp.float32)[:, None]
            return emb
        key = jax.random.key(seed)
        k = jax.random.split(key, 12)
        inp = {'node_feats': jax.random.normal(k[0], (N, 4 * MUL), dtype=jnp.float32), 'edge_vec': jax.random.normal(k[1], (E, 3), dtype=jnp.float32), 'edge_length': jax.random.uniform(k[2], (E,), dtype=jnp.float32), 'senders': jax.random.randint(k[3], (E,), 0, N, dtype=jnp.int32), 'receivers': jax.random.randint(k[4], (E,), 0, N, dtype=jnp.int32), 'num_nodes': N, 'W_up0': jax.random.normal(k[5], (MUL, MUL), dtype=jnp.float32), 'W_up1': jax.random.normal(k[6], (MUL, MUL), dtype=jnp.float32), 'mlp_w0': jax.random.normal(k[7], (NB, 64), dtype=jnp.float32) / NB ** 0.5, 'mlp_b0': jnp.zeros((64,), dtype=jnp.float32), 'mlp_w1': jax.random.normal(k[8], (64, 64), dtype=jnp.float32) / 8.0, 'mlp_b1': jnp.zeros((64,), dtype=jnp.float32), 'mlp_w2': jax.random.normal(k[9], (64, 4 * MUL), dtype=jnp.float32) / 8.0, 'mlp_b2': jnp.zeros((4 * MUL,), dtype=jnp.float32), 'W_out0': jax.random.normal(k[10], (2 * MUL, MUL), dtype=jnp.float32), 'W_out1': jax.random.normal(k[11], (2 * MUL, MUL), dtype=jnp.float32)}
        return inp
    _L2_gnn_all = _L2_gnn_setup()
    _L2_gnn_in = {k: v for k, v in _L2_gnn_all.items() if k in ('W_up0', 'W_up1', 'mlp_w0', 'mlp_b0', 'mlp_w1', 'mlp_b1', 'mlp_w2', 'mlp_b2', 'W_out0', 'W_out1')}
    del _L2_gnn_all

    def _L3_gnn_setup():
        import jax, jax.numpy as jnp
        import numpy as np
        N_NODES = 12500
        N_EDGES = 200000
        D = 128
        LN_EPS = 1e-05
        key = jax.random.key(seed)
        k_x, k_e, k_w, k_b = jax.random.split(key, 4)
        x = jax.random.normal(k_x, (N_NODES, D), dtype=jnp.float32)
        edge_index = jax.random.randint(k_e, (2, N_EDGES), 0, N_NODES, dtype=jnp.int32)
        W = jax.random.normal(k_w, (D, D), dtype=jnp.float32) / np.sqrt(D)
        bias = jax.random.normal(k_b, (D,), dtype=jnp.float32) * 0.02
        ln_gamma = jnp.ones((D,), dtype=jnp.float32)
        ln_beta = jnp.zeros((D,), dtype=jnp.float32)
        return {'x': x, 'edge_index': edge_index, 'W': W, 'bias': bias, 'ln_gamma': ln_gamma, 'ln_beta': ln_beta}
    _L3_gnn_all = _L3_gnn_setup()
    _L3_gnn_in = {k: v for k, v in _L3_gnn_all.items() if k in ('W', 'bias', 'ln_gamma', 'ln_beta')}
    del _L3_gnn_all
    return {'x': x, 'src': src, 'dst': dst, 'edge_attr_3': edge_attr_3, 'edge_weight': edge_weight, 'L0_gnn_W': _L0_gnn_in['W'], 'L0_gnn_attn_l': _L0_gnn_in['attn_l'], 'L0_gnn_attn_r': _L0_gnn_in['attn_r'], 'L0_gnn_bias': _L0_gnn_in['bias'], 'L0_gnn_Wo': _L0_gnn_in['Wo'], 'L0_gnn_bo': _L0_gnn_in['bo'], 'L0_gnn_gamma': _L0_gnn_in['gamma'], 'L0_gnn_beta': _L0_gnn_in['beta'], 'L1_gnn_weight': _L1_gnn_in['weight'], 'L1_gnn_lin1_w': _L1_gnn_in['lin1_w'], 'L1_gnn_lin1_b': _L1_gnn_in['lin1_b'], 'L1_gnn_lin2_w': _L1_gnn_in['lin2_w'], 'L1_gnn_lin2_b': _L1_gnn_in['lin2_b'], 'L2_gnn_W_up0': _L2_gnn_in['W_up0'], 'L2_gnn_W_up1': _L2_gnn_in['W_up1'], 'L2_gnn_mlp_w0': _L2_gnn_in['mlp_w0'], 'L2_gnn_mlp_b0': _L2_gnn_in['mlp_b0'], 'L2_gnn_mlp_w1': _L2_gnn_in['mlp_w1'], 'L2_gnn_mlp_b1': _L2_gnn_in['mlp_b1'], 'L2_gnn_mlp_w2': _L2_gnn_in['mlp_w2'], 'L2_gnn_mlp_b2': _L2_gnn_in['mlp_b2'], 'L2_gnn_W_out0': _L2_gnn_in['W_out0'], 'L2_gnn_W_out1': _L2_gnn_in['W_out1'], 'L3_gnn_W': _L3_gnn_in['W'], 'L3_gnn_bias': _L3_gnn_in['bias'], 'L3_gnn_ln_gamma': _L3_gnn_in['ln_gamma'], 'L3_gnn_ln_beta': _L3_gnn_in['ln_beta']}

def reference(x, src, dst, edge_attr_3, edge_weight, L0_gnn_W, L0_gnn_attn_l, L0_gnn_attn_r, L0_gnn_bias, L0_gnn_Wo, L0_gnn_bo, L0_gnn_gamma, L0_gnn_beta, L1_gnn_weight, L1_gnn_lin1_w, L1_gnn_lin1_b, L1_gnn_lin2_w, L1_gnn_lin2_b, L2_gnn_W_up0, L2_gnn_W_up1, L2_gnn_mlp_w0, L2_gnn_mlp_b0, L2_gnn_mlp_w1, L2_gnn_mlp_b1, L2_gnn_mlp_w2, L2_gnn_mlp_b2, L2_gnn_W_out0, L2_gnn_W_out1, L3_gnn_W, L3_gnn_bias, L3_gnn_ln_gamma, L3_gnn_ln_beta):
    import jax
    import jax.numpy as jnp

    def _L0_gnn_ref(x, src, dst, W, attn_l, attn_r, bias, Wo, bo, gamma, beta):
        import jax, jax.numpy as jnp
        import numpy as np
        N = 6250
        E = 200000
        IN = 128
        H = 4
        F = 32
        D = H * F
        h = (x @ W).reshape(-1, H, F)
        el = (h * attn_l).sum(-1)
        er = (h * attn_r).sum(-1)
        e = jax.nn.leaky_relu(el[src] + er[dst], 0.2)
        emax = jax.ops.segment_max(e, dst, num_segments=N)
        ee = jnp.exp(e - emax[dst])
        denom = jax.ops.segment_sum(ee, dst, num_segments=N)
        alpha = ee / denom[dst]
        msg = h[src] * alpha[:, :, None]
        rst = jax.ops.segment_sum(msg, dst, num_segments=N)
        out = rst.reshape(-1, D) + bias
        out = out @ Wo + bo
        mean = out.mean(0)
        var = out.var(0)
        return (out - mean) / jnp.sqrt(var + 1e-05) * gamma + beta

    def _L1_gnn_ref(x, edge_index, edge_weight, weight, lin1_w, lin1_b, lin2_w, lin2_b):
        import jax, jax.numpy as jnp
        import numpy as np
        N_NODES = 6250
        N_EDGES = 100000
        IN_CH = 128
        OUT_CH = 128
        num_nodes = x.shape[0]
        row, col = (edge_index[0], edge_index[1])
        ew = jnp.where(row == col, jnp.zeros((), x.dtype), edge_weight)
        h = x @ weight
        deg = jax.ops.segment_sum(ew, row, num_segments=num_nodes)
        h_j = ew[:, None] * h[col]
        aggr_out = jax.ops.segment_sum(h_j, row, num_segments=num_nodes)
        out = deg[:, None] * (x @ lin1_w.T + lin1_b) + aggr_out + (x @ lin2_w.T + lin2_b)
        return out

    def _L2_gnn_ref(node_feats, edge_vec, edge_length, senders, receivers, num_nodes, W_up0, W_up1, mlp_w0, mlp_b0, mlp_w1, mlp_b1, mlp_w2, mlp_b2, W_out0, W_out1):
        import jax, jax.numpy as jnp
        import numpy as np
        N = 6250
        E = 100000
        MUL = 32
        NB = 8
        R_MAX = 1.0
        AVG = 16.0
        SQ3 = 3.0 ** 0.5

        def _radial_embedding(r):
            x = jnp.clip(r / R_MAX, 0.0, 1.0)
            centers = jnp.arange(NB, dtype=jnp.float32) / (NB - 1)
            sigma = 1.0 / (NB - 1)
            emb = jnp.exp(-0.5 * ((x[:, None] - centers[None, :]) / sigma) ** 2)
            emb = emb * NB ** 0.5 * (r <= R_MAX).astype(jnp.float32)[:, None]
            return emb
        f32 = jnp.float32
        rhat = edge_vec / (jnp.linalg.norm(edge_vec, axis=-1, keepdims=True) + 1e-12)
        Y1 = SQ3 * rhat
        emb = _radial_embedding(edge_length)
        h = jax.nn.silu(emb @ mlp_w0 + mlp_b0)
        h = jax.nn.silu(h @ mlp_w1 + mlp_b1)
        w = (h @ mlp_w2 + mlp_b2).reshape(-1, 4, MUL)
        s = node_feats[:, :MUL]
        v = node_feats[:, MUL:].reshape(-1, MUL, 3)
        xs = s @ W_up0 / f32(MUL) ** 0.5
        xv = jnp.einsum('nmc,mk->nkc', v, W_up1) / f32(MUL) ** 0.5
        ss = xs[senders]
        vv = xv[senders]
        m0 = w[:, 0] * ss
        m1 = w[:, 1][:, :, None] * ss[:, :, None] * Y1[:, None, :]
        m2 = w[:, 2][:, :, None] * vv
        m3 = w[:, 3] * (jnp.einsum('emc,ec->em', vv, Y1) / SQ3)
        mid_s = jnp.concatenate([m0, m3], axis=1)
        mid_v = jnp.concatenate([m1, m2], axis=1)
        msg_s = jax.ops.segment_sum(mid_s, receivers, num_segments=num_nodes)
        msg_v = jax.ops.segment_sum(mid_v, receivers, num_segments=num_nodes)
        out_s = msg_s @ W_out0 / f32(2 * MUL) ** 0.5
        out_v = jnp.einsum('nmc,mk->nkc', msg_v, W_out1) / f32(2 * MUL) ** 0.5
        out = jnp.concatenate([out_s, out_v.reshape(-1, 3 * MUL)], axis=1)
        return out / max(AVG, 1e-08)

    def _L3_gnn_ref(x, edge_index, W, bias, ln_gamma, ln_beta):
        import jax, jax.numpy as jnp
        import numpy as np
        N_NODES = 12500
        N_EDGES = 200000
        D = 128
        LN_EPS = 1e-05
        N = x.shape[0]
        h = x @ W
        loops = jnp.arange(N, dtype=edge_index.dtype)
        src = jnp.concatenate([edge_index[0], loops])
        dst = jnp.concatenate([edge_index[1], loops])
        deg = jax.ops.segment_sum(jnp.ones_like(src, dtype=h.dtype), dst, num_segments=N)
        dinv = jnp.where(deg > 0, jax.lax.rsqrt(deg), 0.0)
        norm = dinv[src] * dinv[dst]
        agg = jax.ops.segment_sum(h[src] * norm[:, None], dst, num_segments=N)
        agg = agg + bias
        mu = jnp.mean(agg, axis=-1, keepdims=True)
        var = jnp.mean(jnp.square(agg - mu), axis=-1, keepdims=True)
        y = (agg - mu) * jax.lax.rsqrt(var + LN_EPS) * ln_gamma + ln_beta
        y = jax.nn.relu(y)
        return y + x
    edge_index = jnp.stack([src, dst])
    h = jnp.maximum(_layernorm(x, axis=-1), 0.0)
    x = x + _L0_gnn_ref(h, src, dst, L0_gnn_W, L0_gnn_attn_l, L0_gnn_attn_r, L0_gnn_bias, L0_gnn_Wo, L0_gnn_bo, L0_gnn_gamma, L0_gnn_beta)
    h = jnp.maximum(_layernorm(x, axis=-1), 0.0)
    x = x + _L1_gnn_ref(h, edge_index, edge_weight, L1_gnn_weight, L1_gnn_lin1_w, L1_gnn_lin1_b, L1_gnn_lin2_w, L1_gnn_lin2_b)
    h = jnp.maximum(_layernorm(x, axis=-1), 0.0)
    x = x + _L2_gnn_ref(h, edge_attr_3, edge_weight, src, dst, 6250, L2_gnn_W_up0, L2_gnn_W_up1, L2_gnn_mlp_w0, L2_gnn_mlp_b0, L2_gnn_mlp_w1, L2_gnn_mlp_b1, L2_gnn_mlp_w2, L2_gnn_mlp_b2, L2_gnn_W_out0, L2_gnn_W_out1)
    h = jnp.maximum(_layernorm(x, axis=-1), 0.0)
    x = x + _L3_gnn_ref(h, edge_index, L3_gnn_W, L3_gnn_bias, L3_gnn_ln_gamma, L3_gnn_ln_beta)
    return x

_drawn_inputs = setup_inputs


def setup_inputs(seed=0):
    import zlib

    import numpy as np

    out = dict(_drawn_inputs(seed))
    spreads = {'L0_gnn_bias': (0.0, 0.8),
     'L0_gnn_bo': (0.0, 0.8),
     'L0_gnn_gamma': (1.0, 0.2),
     'L0_gnn_beta': (0.0, 0.1),
     'L2_gnn_mlp_b0': (0.0, 0.8),
     'L2_gnn_mlp_b1': (0.0, 0.8),
     'L2_gnn_mlp_b2': (0.0, 0.8),
     'L3_gnn_ln_gamma': (1.0, 0.6),
     'L3_gnn_ln_beta': (0.0, 0.8)}
    factors = {'edge_attr_3': 6.726,
     'L1_gnn_lin2_b': 8.0,
     'L2_gnn_W_up0': 3.086,
     'L2_gnn_W_out0': 3.59,
     'L3_gnn_bias': 8.0}
    for name, (base, spread) in spreads.items():
        noise = np.random.default_rng([zlib.crc32(name.encode()), seed]).standard_normal(out[name].shape)
        drawn = base * np.exp(spread * noise) if base else spread * noise
        out[name] = jnp.asarray(drawn.astype(out[name].dtype))
    for name, factor in factors.items():
        out[name] = (out[name] * factor).astype(out[name].dtype)
    return out
```

```python
import concourse.bass as bass
from concourse import mybir
from contextlib import ExitStack
import numpy as np

F32, BF16, I32 = mybir.dt.float32, mybir.dt.bfloat16, mybir.dt.int32
ALU = mybir.AluOpType
ACT = mybir.ActivationFunctionType
AX = mybir.AxisListType.X

P = 128
N = 6250
E = 206250
C = 128
H, F = 4, 32
NB = 8
HID = 64
TN = (N + P - 1) // P
NPAD = (TN + 1) * P
TG = 7
U = 4
B0 = 16
T = 102 * B0
GROUPS = T // U
EDGE_GROUPS = -(-E // (P * U))
LOOP = -(-E // (P * U * 2))
BATCH2 = T // (2 * B0)
W0 = 2 * H + C
W1 = C + 1
COPIES = 2 * U
BIG = 1e30
EPS = 1e-5
CI, CJ, CT, CH, CM, CP, CR, CO, CEND = 0, 128, 256, 384, 512, 528, 529, 530, 658
RQ = 12
RG = GROUPS // RQ
RH = RG // 2


def constants():
    k = np.zeros((P, CEND), np.float32)
    k[:, CI:CJ] = np.eye(P)
    k[:, CJ:CT] = np.arange(P)[None, :]
    k[:, CT:CH] = np.arange(P)[None, :] < np.arange(P)[:, None]
    rows = np.arange(H * B0)
    k[:H * B0, CH:CM] = (rows[:, None] // B0) == (np.arange(P)[None, :] // F)
    k[:H * B0, CM:CP] = (rows[:, None] % B0) == np.arange(B0)[None, :]
    k[:, CP] = TN * P + np.arange(P)
    k[:NB * RQ, CR] = -(np.arange(NB * RQ) // RQ)
    k[0:3, CO:CEND] = 1.0
    return k


class Chain:

    def __init__(self, eng, sem):
        self.eng, self.sem, self.done, self.step, self.per = eng, sem, 0, None, 0

    def loop(self, step, per):
        self.step, self.per, self.n = step, per, 0

    def end(self, times):
        assert self.n == self.per, (self.n, self.per)
        self.done += times * self.per
        self.step = None

    def __call__(self, ins):
        ins.then_inc(self.sem, 1)
        if self.step is None:
            self.done += 1
            self.eng.wait_ge(self.sem, self.done)
        else:
            self.n += 1
            self.eng.wait_ge(self.sem, self.step * self.per + (self.done + self.n))


def wait_over(eng, sem, value):
    if not isinstance(value, int) or value > 0:
        eng.wait_ge(sem, value)


def peeled(eng, times, step):
    step(0)
    with eng.Fori(1, times) as g:
        step(g)


def ring(eng, total, slots, step):
    with eng.Fori(0, total // slots) as g:
        for r in range(slots):
            step(slots * g + r, g, r)
    for n in range(total - total % slots, total):
        step(n, n // slots, n % slots)


def uses(total, slots, r):
    return (total - r + slots - 1) // slots


def build(nc, a, out):
    ctx = ExitStack()

    def dram(name, shape, dt=F32):
        return nc.dram_tensor(name, shape, dt, kind="Internal").ap()

    table0 = dram("table0", [NPAD, W0])
    table1 = dram("table1", [NPAD, W1])
    table2 = dram("table2", [NPAD, C])
    table3 = dram("table3", [NPAD, C])
    sums1 = [dram(f"sums1_{i}", [NPAD, W1]) for i in range(COPIES)]
    src_f = dram("src_f", [T, P])
    dst_f = dram("dst_f", [T, P])
    basis = dram("basis", [GROUPS, 2, NB, 2 * P])
    count_d = dram("count_d", [NPAD])

    used_sems = []

    with ctx:
        def clear_semaphores():
            with nc.Block() as block:
                @block.gpsimd
                def _(pool):
                    for each in used_sems:
                        pool.sem_clear(each)
            used_sems.clear()

        def alloc(stack):
            def sb(name, shape, dt=F32):
                return stack.enter_context(nc.sbuf_tensor(name, shape, dt))

            def ps(name, shape, dt=F32):
                return stack.enter_context(nc.psum_tensor(name, shape, dt))

            def one_sem(name):
                used_sems.append(stack.enter_context(nc.semaphore(name)))
                return used_sems[-1]

            def sem(name, n=None):
                return one_sem(name) if n is None else [one_sem(f"{name}{i}") for i in range(n)]
            return sb, ps, sem

        sb, _, _ = alloc(ctx)

        def pool_sems(name, n):
            return [ctx.enter_context(nc.semaphore(f"{name}{i}")) for i in range(n)]

        gathered0, scattered1 = pool_sems("gathered0_", 4), pool_sems("scattered1_", 2 * U)
        gathered2, gathered3 = pool_sems("gathered2_", 4), pool_sems("gathered3_", 4)
        K = sb("K", [P, CEND])
        X = sb("X", [P, TN, C])
        HN = sb("HN", [P, NPAD])
        ACC = sb("ACC", [P, 2, NPAD])
        SRC = sb("SRC", [P, T])
        REL = sb("REL", [P, T])
        DINV = sb("DINV", [P, TN])
        D0 = sb("D0", [1, T], I32)
        ident = K[:, CI:CJ]
        lane = K[:, CJ:CT]

        def nodes(table, width):
            return table[0:TN * P, :].rearrange("(t p) c -> p t c", p=P)[:, :, 0:width]

        def one_hots(dst, n):
            return nc.vector.tensor_tensor(
                dst, lane.unsqueeze(1).to_broadcast([P, dst.shape[1], P]),
                REL[:, bass.ds(n * dst.shape[1], dst.shape[1])].unsqueeze(2).to_broadcast([P, dst.shape[1], P]),
                ALU.is_equal)

        def window(eng, tile):
            return eng.value_load(D0[0:1, bass.ds(tile, 1)], min_val=0, max_val=N)

        def flat(ap):
            return ap.rearrange("t e -> (t e)").rearrange("(p k) -> p k", p=P)

        with ExitStack() as st:
            sb, ps, sem = alloc(st)
            dst_i = sb("dst_i", [P, T], I32)
            src_i = sb("src_i", [P, T], I32)
            dcol_i = sb("dcol_i", [P, T], I32)
            scol_i = sb("scol_i", [P, T], I32)
            first_i = sb("first_i", [P, T], I32)
            radius = ACC[0:NB * RQ, :, :].rearrange("p b n -> p (b n)")[:, 0:RH * U * P]
            cutoff = sb("cutoff", [NB * RQ, RH * U * P])
            dst_v, src_v, first_v = HN[:, 0:T], HN[:, T:2 * T], HN[:, 2 * T:3 * T]
            s_in, s_x, s_pad, s_float, s_out, s_chain, s_len, s_clip, s_exp, s_act, s_basis, s_stored = (sem(n) for n in (
                "s_in", "s_x", "s_pad", "s_float", "s_out", "s_chain", "s_len", "s_clip", "s_exp", "s_act", "s_basis", "s_stored"))
            with nc.Block() as block:
                @block.sync
                def _(sp):
                    sp.dma_start(K[:, :], a["consts"]).then_inc(s_in, 16)
                    sp.dma_start(dst_i[:, :], flat(a["dst_rows"])).then_inc(s_in, 16)
                    sp.dma_start(src_i[:, :], flat(a["src_rows"])).then_inc(s_in, 16)
                    sp.dma_start(dcol_i[:, :], a["dst_cols"]).then_inc(s_in, 16)
                    sp.dma_start(scol_i[:, :], a["src_cols"]).then_inc(s_in, 16)
                    sp.dma_start(first_i[:, :], a["dst_first"].to_broadcast([P, T])).then_inc(s_in, 16)
                    sp.dma_start(D0[:, :], a["dst_first"]).then_inc(s_in, 16)
                    sp.dma_start(X[:, 0:TN - 1, :], a["x"][0:(TN - 1) * P, :].rearrange("(t p) c -> p t c", p=P)).then_inc(s_x, 16)
                    sp.wait_ge(s_pad, 1)
                    sp.dma_start(X[0:N - (TN - 1) * P, TN - 1, :], a["x"][(TN - 1) * P:N, :]).then_inc(s_x, 16)
                    sp.wait_ge(s_float, 2)
                    sp.dma_start(flat(dst_f), dst_v).then_inc(s_out, 16)
                    sp.dma_start(flat(src_f), src_v).then_inc(s_out, 16)
                    sp.wait_ge(s_out, 32)
                    sp.wait_ge(s_x, 32)

                @block.scalar
                def _(act):
                    lengths = a["weight_rows"].rearrange("t e -> (t e)").rearrange("(q k) -> q k", q=RQ)
                    groups = basis.rearrange("(q f g) h i e -> q f g h i e", q=RQ, f=2)
                    for half in range(2):
                        if half:
                            act.wait_ge(s_stored, 16 * 2 * NB)
                        for i in range(NB):
                            act.dma_start(radius[i * RQ:(i + 1) * RQ, :],
                                          lengths[:, half * RH * U * P:(half + 1) * RH * U * P]).then_inc(s_len, 16)
                        act.wait_ge(s_in, 16 * 7)
                        act.wait_ge(s_clip, half + 1)
                        nc.scalar.activation(radius, radius, ACT.Square, bias=K[0:NB * RQ, CR:CR + 1],
                                             scale=float(NB - 1)).then_inc(s_act, 1)
                        act.wait_ge(s_act, half + 1)
                        nc.scalar.activation(radius, radius, ACT.Exp, scale=-0.5).then_inc(s_exp, 1)
                        act.wait_ge(s_basis, half + 1)
                        for i in range(NB):
                            for h in range(2):
                                act.dma_start(
                                    groups[:, half, :, h, i, :],
                                    radius[i * RQ:(i + 1) * RQ, :].rearrange("q (g h e) -> q g h e", g=RH, h=2)[:, :, h, :]
                                ).then_inc(s_stored, 16)
                    act.wait_ge(s_stored, 16 * 2 * 2 * NB)

                @block.vector
                def _(dve):
                    link = Chain(dve, s_chain)
                    nc.vector.memset(X[:, TN - 1, :], 0.0).then_inc(s_pad, 1)
                    dve.wait_ge(s_in, 16 * 7)
                    nc.vector.tensor_copy(dst_v, dst_i[:, :]).then_inc(s_float, 1)
                    nc.vector.tensor_copy(src_v, src_i[:, :]).then_inc(s_float, 1)
                    nc.vector.tensor_copy(SRC[:, :], scol_i[:, :])
                    nc.vector.tensor_copy(REL[:, :], dcol_i[:, :])
                    link(nc.vector.tensor_copy(first_v, first_i[:, :]))
                    link(nc.vector.tensor_tensor(REL[:, :], REL[:, :], first_v, ALU.subtract))
                    for half in range(2):
                        dve.wait_ge(s_len, 16 * NB * (half + 1))
                        link(nc.vector.tensor_scalar(cutoff[:, :], radius, 1.0, float(NB ** 0.5), ALU.is_le, ALU.mult))
                        nc.vector.tensor_scalar(radius, radius, 0.0, 1.0, ALU.max, ALU.min).then_inc(s_clip, 1)
                        dve.wait_ge(s_exp, half + 1)
                        nc.vector.tensor_tensor(radius, radius, cutoff[:, :], ALU.mult).then_inc(s_basis, 1)

        def node_stage(L, width, table, load, n_load, prepare, ones=0, extra=None, scale=None, clear=False):
            with ExitStack() as st:
                sb, ps, sem = alloc(st)
                hn = HN[:, 0:TN * C].rearrange("p (t c) -> p t c", t=TN)
                TAB = sb(f"TAB{L}", [P, TN, width + ones])
                sq = TAB[:, :, 0:C]
                WT = sb(f"WT{L}", [P, width])
                WX = sb(f"WX{L}", [P, 2 * C])
                mean = sb(f"mean{L}", [P, TN])
                var = sb(f"var{L}", [P, TN])
                turn = sb(f"turn{L}", [P, TG, C])
                turned = sb(f"turned{L}", [P, TG, C])
                psT = ps(f"psT{L}", [P, 8, C])
                psM = ps(f"psM{L}", [P, 8, 2 * C])
                s_w, s_chain, s_var, s_sqrt, s_rows, s_t, s_ht, s_prod, s_tab, s_done, s_ones, s_out = (sem(f"{n}_{L}") for n in (
                    "s_w", "s_chain", "s_var", "s_sqrt", "s_rows", "s_t", "s_ht", "s_prod", "s_tab", "s_done", "s_ones", "s_out"))
                s_clear = sem(f"s_clear_{L}")
                steps = TN // TG
                with nc.Block() as block:
                    @block.sync
                    def _(sp):
                        if clear:
                            sp.wait_ge(s_clear, 1)
                        load(sp, WT, WX, s_w)
                        sp.wait_ge(s_w, 16 * n_load)
                        sp.wait_ge(s_done, steps)
                        if ones:
                            sp.wait_ge(s_ones, 1)
                        sp.dma_start(table[0:TN * P, :].rearrange("(t p) c -> p t c", p=P), TAB[:, :, :]).then_inc(s_out, 16)
                        sp.dma_start(table[TN * P:NPAD, :], TAB[:, 0, :]).then_inc(s_out, 16)
                        sp.wait_ge(s_out, 32)

                    @block.vector
                    def _(dve):
                        link = Chain(dve, s_chain)
                        if clear:
                            nc.vector.memset(WX[:, :], 0.0).then_inc(s_clear, 1)
                        dve.wait_ge(s_w, 16 * n_load)
                        prepare(link, WT, WX)
                        link(nc.vector.reduce_sum(mean[:, :], X[:, :, :], axis=AX))
                        link(nc.vector.tensor_scalar(mean[:, :], mean[:, :], 1.0 / C, None, ALU.mult))
                        link(nc.vector.tensor_tensor(hn, X[:, :, :], mean[:, :].unsqueeze(2).to_broadcast([P, TN, C]), ALU.subtract))
                        link(nc.vector.tensor_tensor(sq, hn, hn, ALU.mult))
                        link(nc.vector.reduce_sum(var[:, :], sq, axis=AX))
                        nc.vector.tensor_scalar(var[:, :], var[:, :], 1.0 / C, EPS, ALU.mult, ALU.add).then_inc(s_var, 1)
                        dve.wait_ge(s_sqrt, 1)
                        link(nc.vector.reciprocal(var[:, :], var[:, :]))
                        link(nc.vector.tensor_tensor(hn, hn, var[:, :].unsqueeze(2).to_broadcast([P, TN, C]), ALU.mult))
                        if ones:
                            nc.vector.memset(TAB[:, :, width:width + ones], 1.0).then_inc(s_ones, 1)
                        nc.vector.tensor_scalar(turn[:, :, :], hn[:, 0:TG, :], 0.0, None, ALU.max).then_inc(s_rows, 1)

                        def store(at):
                            if extra is not None:
                                nc.vector.tensor_copy(extra[:, at, 0:C], psM[:, 0:TG, C:2 * C])
                                nc.vector.tensor_copy(extra[:, at, C:2 * C], psT[:, 0:TG, :])
                            if scale is None:
                                nc.vector.tensor_copy(TAB[:, at, 0:width], psM[:, 0:TG, 0:width]).then_inc(s_done, 1)
                            else:
                                nc.vector.tensor_tensor(TAB[:, at, 0:width], psM[:, 0:TG, 0:width],
                                                        scale[:, at].unsqueeze(2).to_broadcast([P, TG, width]), ALU.mult).then_inc(s_done, 1)

                        with dve.Fori(0, steps - 1) as g:
                            dve.wait_ge(s_t, g + 1)
                            nc.vector.tensor_scalar(turn[:, :, :], hn[:, bass.ds((g + 1) * TG, TG), :], 0.0, None, ALU.max).then_inc(s_rows, 1)
                            dve.wait_ge(s_prod, g + 1)
                            store(bass.ds(g * TG, TG))
                        dve.wait_ge(s_prod, steps)
                        store(slice((steps - 1) * TG, TN))

                    @block.scalar
                    def _(act):
                        act.wait_ge(s_var, 1)
                        nc.scalar.activation(var[:, :], var[:, :], ACT.Sqrt).then_inc(s_sqrt, 1)
                        with act.Fori(0, steps) as g:
                            act.wait_ge(s_t, g + 1)
                            nc.scalar.copy(turned[:, :, :], psT[:, 0:TG, :]).then_inc(s_ht, 1)

                    @block.tensor
                    def _(pe):
                        with pe.Fori(0, steps) as g:
                            pe.wait_ge(s_rows, g + 1)
                            for i in range(TG):
                                last = nc.tensor.transpose(psT[:, i, :], turn[:, i, :], ident)
                            last.then_inc(s_t, 1)
                            pe.wait_ge(s_ht, g + 1)
                            for i in range(TG):
                                if extra is None:
                                    last = nc.tensor.matmul(psM[:, i, 0:width], turned[:, i, :], WT[:, :], start=True, stop=True)
                                else:
                                    nc.tensor.matmul(psM[:, i, 0:C], turned[:, i, :], WT[:, :], start=True, stop=True)
                                    nc.tensor.matmul(psM[:, i, C:2 * C], turned[:, i, :], WX[:, 0:C], start=True, stop=True)
                                    last = nc.tensor.matmul(psT[:, i, :], turned[:, i, :], WX[:, C:2 * C], start=True, stop=True)
                            last.then_inc(s_prod, 1)
                            pe.wait_ge(s_done, g + 1)

        def load0(sp, WT, WX, s_w):
            sp.dma_start(WT[:, 0:C], a["L0_gnn_W"]).then_inc(s_w, 16)
            for i, name in enumerate(("L0_gnn_attn_l", "L0_gnn_attn_r")):
                row = a[name].rearrange("h f -> (h f)").unsqueeze(0)
                sp.dma_start(WX[:, i * C:(i + 1) * C], row.to_broadcast([P, C])).then_inc(s_w, 16)

        def prepare0(link, WT, WX):
            for i in range(2):
                part = WX[:, i * C:(i + 1) * C]
                link(nc.vector.tensor_tensor(part, WT[:, 0:C], part, ALU.mult))
                link(nc.vector.reduce_sum(WT[:, C + i * H:C + (i + 1) * H], part.rearrange("p (h f) -> p h f", h=H), axis=AX))

        node_stage(0, W0, table0, load0, 3, prepare0)

        with ExitStack() as st:
            sb, ps, sem = alloc(st)
            R0 = H * B0
            CNT = HN[0:1, :]
            index = sb("index0", [P, 2, B0], I32)
            rows = sb("rows0", [P, 2, B0, W0])
            er = sb("er0", [P, 2, B0, H])
            hot = sb("hot0", [P, B0, P])
            hotT = sb("hotT0", [P, B0, P])
            drow = sb("drow0", [R0, 2, P])
            cut = sb("cut0", [R0, P + 1])
            score = sb("score0", [P, H, B0])
            scoreR = sb("scoreR0", [R0, P])
            low = sb("low0", [R0, P])
            top = sb("top0", [R0, P])
            shifted = sb("shifted0", [R0, P + 1])
            carryC = sb("carryC0", [R0, 1])
            tail = sb("tail0", [1, R0])
            run = sb("run0", [1, H, B0 + 1])
            carry = sb("carry0", [1, H, B0])
            prob = sb("prob0", [P, B0, H, F])
            fadeL = sb("fadeL0", [R0, P])
            fade = sb("fade0", [P, B0])
            sameR = sb("sameR", [1, T])
            sameC = sb("sameC", [1, T])
            lasts = rows[0:1, :, :, :].rearrange("o s t c -> o (s t c)").bitcast(I32)[:, 0:T]
            first_f = hot[0:1, :, :].rearrange("o t e -> o (t e)")[:, 0:T]
            last_f = hotT[0:1, :, :].rearrange("o t e -> o (t e)")[:, 0:T]
            zero = sb("zero", [P, W1])
            one_col = sb("one_col", [P, 1], BF16)
            hotB = sb("hotB", [P, B0, P], BF16)
            psH = ps("psH0", [P, 2, 4, P])
            psE = ps("psE0", [P, 512])
            psS = ps("psS0", [R0, 512])
            psB = ps("psB0", [P, 512])
            psA = ps("psA0", [P, 2, 4, P])
            names = ("s_last", "s_ready", "s_hot", "s_turn", "s_hotT", "s_er", "s_score", "s_scoreR", "s_low", "s_tail",
                     "s_carry", "s_carryC", "s_shift", "s_exp", "s_probR", "s_fadeL", "s_fade", "s_msg", "s_sum", "s_free",
                     "s_batch", "s_chain", "s_out")
            s_prob, s_zero, s_clear = sem("s_prob_e0"), sem("s_zero_e0"), sem("s_clear_e0")
            (s_last, s_ready, s_hot, s_turn, s_hotT, s_er, s_score, s_scoreR, s_low, s_tail, s_carry, s_carryC, s_shift,
             s_exp, s_probR, s_fadeL, s_fade, s_msg, s_sum, s_free, s_batch, s_chain, s_out) = (sem(n + "_e0") for n in names)
            s_rows = gathered0
            s_index, s_erw, s_drow = (sem(n, 2) for n in ("s_index_e0", "s_erw_e0", "s_drow_e0"))
            with nc.Block() as block:
                @block.sync
                def _(sp):
                    sp.dma_start(lasts, a["dst_last"]).then_inc(s_last, 16)
                    with sp.Fori(0, BATCH2) as g:
                        for s in range(2):
                            sp.wait_ge(s_batch, 2 * g + (s + 1))
                            sp.dma_start(index[:, s, :], a["src_batches"][bass.ds(2 * g + s, 1), :, :].rearrange("b p t -> (b p) t")).then_inc(s_index[s], 16)
                            for h in range(H):
                                sp.dma_start(drow[h * B0:(h + 1) * B0, s, :], dst_f[bass.ds((2 * g + s) * B0, B0), :]).then_inc(s_drow[s], 16)
                            for k in range(B0):
                                first = window(sp, (2 * g + s) * B0 + k)
                                sp.dma_start(er[:, s, k, :], table0[bass.ds(first, P), C + H:C + 2 * H]).then_inc(s_erw[s], 16)
                    for s in range(2):
                        sp.wait_ge(s_index[s], 16 * BATCH2)
                        sp.wait_ge(s_drow[s], 16 * H * BATCH2)
                        sp.wait_ge(s_erw[s], 16 * B0 * BATCH2)
                    sp.wait_ge(s_batch, 2 + 2 * BATCH2)
                    sp.dma_start(count_d.unsqueeze(0), CNT[:, :]).then_inc(s_out, 16)
                    sp.wait_ge(s_out, 16)

                @block.gpsimd
                def _(pool):
                    with pool.Fori(0, BATCH2) as g:
                        for s in range(2):
                            pool.wait_ge(s_index[s], 16 * g + 16)
                            pool.nop(nofuse=True)
                            for k in range(B0):
                                nc.gpsimd.indirect_dma_start(
                                    out=rows[:, s, k, :], out_offset=None, in_=table0[:, :],
                                    in_offset=bass.IndirectOffsetOnAxis(ap=index[:, s, k:k + 1], axis=0)).then_inc(s_rows[s], 16)
                    for s in range(2):
                        pool.wait_ge(s_rows[s], 16 * B0 * BATCH2)

                @block.scalar
                def _(act):
                    act.wait_ge(s_zero, 1)
                    for k in range(COPIES):
                        act.dma_start(sums1[k].rearrange("(t p) c -> p t c", p=P), zero[:, :].unsqueeze(1).to_broadcast([P, NPAD // P, W1])).then_inc(s_clear, 16)
                    with act.Fori(0, BATCH2) as g:
                        for s in range(2):
                            for q in range(B0 // 4):
                                act.wait_ge(s_turn, (2 * g + s) * (B0 // 4) + (q + 1))
                                nc.scalar.copy(hotT[:, 4 * q:4 * q + 4, :], psH[:, q % 2, :, :]).then_inc(s_hotT, 1)
                            act.wait_ge(s_shift, 2 * g + (s + 1))
                            nc.scalar.activation(shifted[:, :], shifted[:, :], ACT.Exp).then_inc(s_exp, 1)
                            act.wait_ge(s_probR, 2 * g + (s + 1))
                            act.wait_ge(s_batch, 2 * g + (s + 2))
                            nc.scalar.copy(prob[:, :, :, :], psB[:, 128:128 + R0].rearrange("p (h t) -> p t h", h=H).unsqueeze(3).to_broadcast([P, B0, H, F])).then_inc(s_prob, 1)
                    act.wait_ge(s_clear, 16 * COPIES)

                @block.vector
                def _(dve):
                    link = Chain(dve, s_chain)
                    dve.wait_ge(s_last, 16)
                    link(nc.vector.memset(ACC[:, :, :], 0.0))
                    nc.vector.memset(CNT[:, :], 0.0)
                    nc.vector.memset(one_col[:, :], 1.0)
                    nc.vector.memset(zero[:, :], 0.0).then_inc(s_zero, 1)
                    nc.vector.memset(cut[:, :], 0.0)
                    link(nc.vector.memset(run[:, :, :], -BIG))
                    nc.vector.tensor_copy(first_f, D0[:, :])
                    link(nc.vector.tensor_copy(last_f, lasts))
                    link(nc.vector.memset(sameR[:, :], 1.0))
                    link(nc.vector.memset(sameC[:, :], 1.0))
                    link(nc.vector.tensor_tensor(sameR[:, 1:T], last_f[:, 1:T], last_f[:, 0:T - 1], ALU.not_equal))
                    link(nc.vector.tensor_tensor(sameC[:, 1:T], first_f[:, 1:T], last_f[:, 0:T - 1], ALU.not_equal))
                    link(nc.vector.tensor_scalar(sameR[:, :], sameR[:, :], -BIG, None, ALU.mult))
                    link(nc.vector.tensor_scalar(sameC[:, :], sameC[:, :], -BIG, None, ALU.mult))
                    dve.sem_inc(s_batch, 2)
                    dve.sem_inc(s_free, 2)
                    dve.sem_inc(s_ready, 1)
                    with dve.Fori(0, BATCH2) as g:
                        link.loop(g, 2 * (12 + H + B0))
                        for s in range(2):
                            n = 2 * g + s
                            one_hots(hot[:, :, :], n).then_inc(s_hot, 1)
                            dve.wait_ge(s_hot, n + 1)
                            link(nc.vector.tensor_copy(hotB[:, :, :], hot[:, :, :]))
                            dve.wait_ge(s_drow[s], 16 * H * g + 16 * H)
                            link(nc.vector.tensor_tensor(cut[:, 1:P], drow[:, s, 1:P], drow[:, s, 0:P - 1], ALU.not_equal))
                            link(nc.vector.tensor_scalar(cut[:, 1:P], cut[:, 1:P], -BIG, None, ALU.mult))
                            dve.wait_ge(s_er, n + 1)
                            dve.wait_ge(s_rows[s], 16 * B0 * g + 16 * B0)
                            link(nc.vector.tensor_tensor(score[:, :, :], rows[:, s, :, C:C + H].rearrange("p t h -> p h t"),
                                                         psE[:, 0:R0].rearrange("p (t h) -> p h t", t=B0), ALU.add))
                            nc.vector.scalar_tensor_tensor(score[:, :, :], score[:, :, :], 0.2, score[:, :, :], ALU.mult, ALU.max).then_inc(s_score, 1)
                            dve.wait_ge(s_scoreR, n + 1)
                            link(nc.vector.tensor_copy(scoreR[:, :], psS[:, 0:P]))
                            nc.vector.tensor_tensor_scan(low[:, :], cut[:, 0:P], scoreR[:, :], -BIG, ALU.add, ALU.max).then_inc(s_low, 1)
                            dve.wait_ge(s_tail, n + 1)
                            link(nc.vector.tensor_copy(tail[:, :], psB[0:1, 0:R0]))
                            for h in range(H):
                                link(nc.vector.tensor_tensor_scan(run[:, h, 1:B0 + 1], sameR[:, bass.ds(n * B0, B0)], tail[:, h * B0:(h + 1) * B0],
                                                                  run[:, h, 0:1], ALU.add, ALU.max))
                            nc.vector.tensor_tensor(carry[:, :, :], run[:, :, 0:B0], sameC[:, bass.ds(n * B0, B0)].unsqueeze(1).to_broadcast([1, H, B0]), ALU.add).then_inc(s_carry, 1)
                            dve.wait_ge(s_carry, n + 1)
                            link(nc.vector.tensor_copy(run[:, :, 0:1], run[:, :, B0:B0 + 1]))
                            dve.wait_ge(s_carryC, n + 1)
                            link(nc.vector.tensor_copy(carryC[:, :], psS[:, 256:257]))
                            link(nc.vector.tensor_tensor_scan(low[:, :], cut[:, 0:P], scoreR[:, :], carryC[:, :], ALU.add, ALU.max))
                            link(nc.vector.tensor_tensor_scan(top[:, ::-1], cut[:, P:0:-1], low[:, ::-1], -BIG, ALU.add, ALU.max))
                            link(nc.vector.tensor_tensor(shifted[:, 0:P], scoreR[:, :], top[:, :], ALU.subtract))
                            nc.vector.tensor_tensor(shifted[:, P:P + 1], carryC[:, :], top[:, 0:1], ALU.subtract).then_inc(s_shift, 1)
                            dve.wait_ge(s_exp, n + 1)
                            nc.vector.tensor_scalar(fadeL[:, :], K[0:R0, CH:CM], shifted[:, P:P + 1], None, ALU.mult).then_inc(s_fadeL, 1)
                            dve.wait_ge(s_prob, n + 1)
                            nc.vector.tensor_tensor(rows[:, s, :, 0:C], rows[:, s, :, 0:C], prob[:, :, :, :].rearrange("p t h f -> p t (h f)"),
                                                    ALU.mult).then_inc(s_msg, 1)
                            dve.wait_ge(s_fade, n + 1)
                            link(nc.vector.tensor_copy(fade[:, :], psE[:, 256:256 + B0]))
                            for k in range(B0):
                                first = window(dve, n * B0 + k)
                                dve.wait_ge(s_sum, n * B0 + (k + 1))
                                nc.vector.tensor_tensor(CNT[:, bass.ds(first, P)], CNT[:, bass.ds(first, P)], psA[0:1, k % 2, 2, :], ALU.add)
                                nc.vector.scalar_tensor_tensor(ACC[:, :, bass.ds(first, 1)], ACC[:, :, bass.ds(first, 1)], fade[:, k:k + 1],
                                                               psA[:, k % 2, 0:2, 0:1], ALU.mult, ALU.add)
                                link(nc.vector.tensor_tensor(ACC[:, :, bass.ds(first + 1, P - 1)], ACC[:, :, bass.ds(first + 1, P - 1)],
                                                             psA[:, k % 2, 0:2, 1:P], ALU.add))
                                dve.sem_inc(s_free, 1)
                            dve.sem_inc(s_batch, 1)
                    link.end(BATCH2)

                @block.tensor
                def _(pe):
                    pe.wait_ge(s_ready, 1)
                    with pe.Fori(0, BATCH2) as g:
                        for s in range(2):
                            n = 2 * g + s
                            pe.wait_ge(s_hot, n + 1)
                            for q in range(B0 // 4):
                                pe.wait_ge(s_hotT, n * (B0 // 4) + (q - 1)) if q >= 2 else None
                                for k in range(4):
                                    last = nc.tensor.transpose(psH[:, q % 2, k, :], hot[:, 4 * q + k, :], ident)
                                last.then_inc(s_turn, 1)
                            pe.wait_ge(s_hotT, (n + 1) * (B0 // 4))
                            pe.wait_ge(s_erw[s], 16 * B0 * g + 16 * B0)
                            for k in range(B0):
                                last = nc.tensor.matmul(psE[:, k * H:(k + 1) * H], hotT[:, k, :], er[:, s, k, :], start=True, stop=True)
                            last.then_inc(s_er, 1)
                            pe.wait_ge(s_score, n + 1)
                            pe.nop(nofuse=True)
                            nc.tensor.transpose(psS[:, 0:P], score[:, :, :].rearrange("p h t -> p (h t)"), ident).then_inc(s_scoreR, 1)
                            pe.wait_ge(s_low, n + 1)
                            pe.nop(nofuse=True)
                            nc.tensor.transpose(psB[0:1, 0:R0], low[:, P - 1:P], ident[0:R0, 0:R0]).then_inc(s_tail, 1)
                            pe.wait_ge(s_carry, n + 1)
                            pe.nop(nofuse=True)
                            nc.tensor.transpose(psS[:, 256:257], carry[:, :, :].rearrange("o h t -> o (h t)"), ident[0:1, 0:1]).then_inc(s_carryC, 1)
                            pe.wait_ge(s_exp, n + 1)
                            pe.nop(nofuse=True)
                            nc.tensor.transpose(psB[:, 128:128 + R0], shifted[:, 0:P], ident[0:R0, 0:R0]).then_inc(s_probR, 1)
                            pe.wait_ge(s_fadeL, n + 1)
                            nc.tensor.matmul(psE[:, 256:256 + B0], fadeL[:, :], K[0:R0, CM:CP], start=True, stop=True).then_inc(s_fade, 1)
                            pe.wait_ge(s_msg, n + 1)
                            for k in range(B0):
                                pe.wait_ge(s_free, n * B0 + (k + 1))
                                nc.tensor.matmul(psA[:, k % 2, 0, :], rows[:, s, k, 0:C], hot[:, k, :], start=True, stop=True)
                                nc.tensor.matmul(psA[:, k % 2, 1, :], prob[:, k, :, :].rearrange("p h f -> p (h f)"), hot[:, k, :], start=True, stop=True)
                                nc.tensor.matmul(psA[0:1, k % 2, 2, :], one_col[:, :], hotB[:, k, :], start=True, stop=True).then_inc(s_sum, 1)

        with ExitStack() as st:
            sb, ps, sem = alloc(st)
            wo = sb("wo", [P, C])
            cols = sb("cols0", [P, 4])
            degree = sb("degree", [P, TN])
            stat = sb("stat0", [P, 4])
            stage = sb("stage0", [P, TG * C])
            psP = ps("psP0", [P, 2, 512])
            psT = ps("psT_f0", [P, 8, C])
            (s_in, s_chain, s_rst, s_proj, s_o, s_free, s_var, s_sqrt, s_deg, s_root, s_stage, s_turn, s_added) = (sem(n + "_f0") for n in (
                "s_in", "s_chain", "s_rst", "s_proj", "s_o", "s_free", "s_var", "s_sqrt", "s_deg", "s_root", "s_stage", "s_turn", "s_added"))
            CH0 = 400
            with nc.Block() as block:
                @block.sync
                def _(sp):
                    sp.dma_start(wo[:, :], a["L0_gnn_Wo"]).then_inc(s_in, 16)
                    for i, name in enumerate(("bias", "bo", "gamma", "beta")):
                        sp.dma_start(cols[:, i:i + 1], a["L0_gnn_" + name].unsqueeze(1)).then_inc(s_in, 16)
                    sp.dma_start(degree[:, :], count_d[0:TN * P].rearrange("(t p) -> p t", p=P), allow_slow_non_contiguous=True).then_inc(s_in, 16)
                    sp.wait_ge(s_in, 16 * 6)

                @block.vector
                def _(dve):
                    link = Chain(dve, s_chain)
                    sums, total = ACC[:, 0, :], ACC[:, 1, :]
                    link(nc.vector.tensor_scalar(total, total, 1e-30, None, ALU.max))
                    link(nc.vector.reciprocal(total, total))
                    link(nc.vector.tensor_tensor(sums, sums, total, ALU.mult))
                    dve.wait_ge(s_in, 16 * 6)
                    nc.vector.tensor_scalar(sums, sums, cols[:, 0:1], None, ALU.add).then_inc(s_rst, 1)
                    nc.vector.tensor_scalar(degree[:, :], degree[:, :], 1.0, None, ALU.add).then_inc(s_deg, 1)
                    with dve.Fori(0, NPAD // CH0 // 2) as g:
                        for s in range(2):
                            dve.wait_ge(s_proj, 2 * g + (s + 1))
                            nc.vector.tensor_scalar(HN[:, bass.ds((2 * g + s) * CH0, CH0)], psP[:, s, 0:CH0], cols[:, 1:2], None, ALU.add).then_inc(s_o, 1)
                    dve.wait_ge(s_o, NPAD // CH0)
                    o = HN[:, 0:N]
                    link(nc.vector.reduce_sum(stat[:, 0:1], o, axis=AX))
                    link(nc.vector.tensor_scalar(stat[:, 0:1], stat[:, 0:1], 1.0 / N, None, ALU.mult))
                    link(nc.vector.tensor_scalar(HN[:, :], HN[:, :], stat[:, 0:1], None, ALU.subtract))
                    link(nc.vector.tensor_tensor(total[:, 0:N], o, o, ALU.mult))
                    link(nc.vector.reduce_sum(stat[:, 1:2], total[:, 0:N], axis=AX))
                    nc.vector.tensor_scalar(stat[:, 1:2], stat[:, 1:2], 1.0 / N, EPS, ALU.mult, ALU.add).then_inc(s_var, 1)
                    dve.wait_ge(s_sqrt, 1)
                    nc.vector.reciprocal(DINV[:, :], degree[:, :])
                    link(nc.vector.reciprocal(stat[:, 1:2], stat[:, 1:2]))
                    link(nc.vector.tensor_tensor(stat[:, 2:3], stat[:, 1:2], cols[:, 2:3], ALU.mult))
                    dve.sem_inc(s_root, 1)
                    with dve.Fori(0, TN // TG) as g:
                        dve.wait_ge(s_turn, g + 1)
                        nc.vector.tensor_tensor(X[:, bass.ds(g * TG, TG), :], X[:, bass.ds(g * TG, TG), :], psT[:, 0:TG, :], ALU.add).then_inc(s_added, 1)

                @block.scalar
                def _(act):
                    act.wait_ge(s_deg, 1)
                    nc.scalar.activation(degree[:, :], degree[:, :], ACT.Sqrt)
                    act.wait_ge(s_var, 1)
                    nc.scalar.activation(stat[:, 1:2], stat[:, 1:2], ACT.Sqrt).then_inc(s_sqrt, 1)
                    act.wait_ge(s_root, 1)
                    with act.Fori(0, TN // TG) as g:
                        nc.scalar.activation(stage[:, :], HN[:, bass.ds(g * TG * C, TG * C)], ACT.Identity, bias=cols[:, 3:4], scale=stat[:, 2:3]).then_inc(s_stage, 1)
                        act.wait_ge(s_turn, g + 1)

                @block.tensor
                def _(pe):
                    pe.wait_ge(s_rst, 1)
                    with pe.Fori(0, NPAD // CH0 // 2) as g:
                        for s in range(2):
                            nc.tensor.matmul(psP[:, s, 0:CH0], wo[:, :], ACC[:, 0, bass.ds((2 * g + s) * CH0, CH0)], start=True, stop=True).then_inc(s_proj, 1)
                        pe.wait_ge(s_o, 2 * g + 2)
                    with pe.Fori(0, TN // TG) as g:
                        pe.wait_ge(s_stage, g + 1)
                        for i in range(TG):
                            last = nc.tensor.transpose(psT[:, i, :], stage[:, i * C:(i + 1) * C], ident)
                        last.then_inc(s_turn, 1)
                        pe.wait_ge(s_added, g + 1)

        clear_semaphores()

        LIN = ACC[:, :, :].rearrange("p b n -> p (b n)")[:, 0:TN * 2 * C].rearrange("p (t c) -> p t c", t=TN)

        def load1(sp, WT, WX, s_w):
            sp.dma_start(WT[:, :], a["L1_gnn_weight"]).then_inc(s_w, 16)
            sp.dma_start(WX[:, 0:C], a["L1_gnn_lin1_w"]).then_inc(s_w, 16)
            sp.dma_start(WX[:, C:2 * C], a["L1_gnn_lin2_w"]).then_inc(s_w, 16)

        node_stage(1, C, table1, load1, 3, lambda link, WT, WX: None, ones=1, extra=LIN)

        with ExitStack() as st:
            sb, ps, sem = alloc(st)
            weight = sb("weight1", [P, T])
            dst_i = sb("dst_i1", [P, T], I32)
            other = sb("other1", [P, T])
            srow = sb("srow1", [P, 2, U, P])
            win = sb("win1", [P, 2, U, W1])
            same = sb("same1", [P, 2, U, P])
            hotW = sb("hotW1", [P, 2, U, P])
            mix = sb("mix1", [P, 2, U, P])
            before = sb("before1", [P, U, P])
            later = sb("later1", [P, U])
            place = sb("place1", [P, U])
            index = sb("index1", [P, 2, U], I32)
            sums = sb("sumrows1", [P, 2, U, W1])
            psX = ps("psX1", [P, 2, U, P])
            psV = ps("psV1", [P, 2, U, 2 * P])
            (s_in, s_chain, s_same, s_hot, s_mix, s_mixed, s_rows, s_index, s_done) = (sem(n + "_e1") for n in (
                "s_in", "s_chain", "s_same", "s_hot", "s_mix", "s_mixed", "s_rows", "s_index", "s_done"))
            s_srow, s_win = (sem(n, 2) for n in ("s_srow_e1", "s_win_e1"))
            s_added = scattered1
            with nc.Block() as block:
                @block.sync
                def _(sp):
                    sp.dma_start(weight[:, :], a["weight_cols"]).then_inc(s_in, 16)
                    sp.dma_start(dst_i[:, :], a["dst_cols"]).then_inc(s_in, 16)
                    with sp.Fori(0, LOOP) as g:
                        for s in range(2):
                            n = 2 * g + s
                            sp.wait_ge(s_done, n + 1)
                            sp.dma_start(srow[:, s, :, :].rearrange("p u e -> p (u e)"), src_f[bass.ds(n * U, U), :].rearrange("t e -> (t e)").unsqueeze(0).to_broadcast([P, U * P])).then_inc(s_srow[s], 16)
                            for u in range(U):
                                first = window(sp, n * U + u)
                                sp.dma_start(win[:, s, u, :], table1[bass.ds(first, P), :]).then_inc(s_win[s], 16)
                    for s in range(2):
                        sp.wait_ge(s_srow[s], 16 * LOOP)
                        sp.wait_ge(s_win[s], 16 * U * LOOP)

                @block.vector
                def _(dve):
                    link = Chain(dve, s_chain)
                    dve.wait_ge(s_in, 32)
                    link(nc.vector.tensor_copy(other[:, :], dst_i[:, :]))
                    link(nc.vector.tensor_tensor(other[:, :], SRC[:, :], other[:, :], ALU.not_equal))
                    link(nc.vector.tensor_tensor(weight[:, :], weight[:, :], other[:, :], ALU.mult))

                    def step(g):
                        link.loop(g, 2 * 5)
                        for s in range(2):
                            n = 2 * g + s
                            dve.wait_ge(s_srow[s], 16 * g + 16)
                            dve.wait_ge(s_done, n + 1)
                            tile_src = SRC[:, bass.ds(n * U, U)]
                            nc.vector.tensor_tensor(same[:, s, :, :], srow[:, s, :, :], tile_src.unsqueeze(2).to_broadcast([P, U, P]), ALU.is_equal).then_inc(s_same, 1)
                            for u in range(U):
                                last = nc.vector.tensor_scalar(hotW[:, s, u, :], lane, REL[:, bass.ds(n * U + u, 1)],
                                                               weight[:, bass.ds(n * U + u, 1)], ALU.is_equal, ALU.mult)
                            last.then_inc(s_hot, 1)
                            dve.wait_ge(s_same, n + 1)
                            link(nc.vector.tensor_tensor(before[:, :, :], same[:, s, :, :], K[:, CT:CH].unsqueeze(1).to_broadcast([P, U, P]), ALU.mult))
                            link(nc.vector.reduce_max(later[:, :], before[:, :, :], axis=AX))
                            link(nc.vector.tensor_scalar(place[:, :], tile_src, -1.0, K[:, CP:CP + 1], ALU.mult, ALU.add))
                            link(nc.vector.tensor_tensor(place[:, :], place[:, :], later[:, :], ALU.mult))
                            link(nc.vector.tensor_tensor(place[:, :], place[:, :], tile_src, ALU.add))
                            for u in range(U):
                                wait_over(dve, s_added[s * U + u], 16 * g)
                            nc.vector.tensor_copy(index[:, s, :], place[:, :]).then_inc(s_index, 1)
                            dve.wait_ge(s_index, n + 1)

                    peeled(dve, LOOP, step)
                    link.end(LOOP)

                @block.scalar
                def _(act):
                    act.sem_inc(s_done, 2)

                    def step(g):
                        for s in range(2):
                            n = 2 * g + s
                            act.wait_ge(s_mix, n + 1)
                            nc.scalar.copy(mix[:, s, :, :], psX[:, s, :, :]).then_inc(s_mixed, 1)
                            act.wait_ge(s_rows, n + 1)
                            for u in range(U):
                                wait_over(act, s_added[s * U + u], 16 * g)
                            nc.scalar.copy(sums[:, s, :, :], psV[:, s, :, 0:W1]).then_inc(s_done, 1)

                    peeled(act, LOOP, step)

                @block.tensor
                def _(pe):
                    with pe.Fori(0, LOOP) as g:
                        for s in range(2):
                            n = 2 * g + s
                            pe.wait_ge(s_hot, n + 1)
                            pe.wait_ge(s_same, n + 1)
                            for u in range(U):
                                last = nc.tensor.matmul(psX[:, s, u, :], hotW[:, s, u, :], same[:, s, u, :], start=True, stop=True)
                            last.then_inc(s_mix, 1)
                            pe.wait_ge(s_win[s], 16 * U * g + 16 * U)
                            pe.wait_ge(s_mixed, n + 1)
                            pe.wait_ge(s_done, n + 1)
                            for u in range(U):
                                last = nc.tensor.matmul(psV[:, s, u, 0:W1], mix[:, s, u, :], win[:, s, u, :], start=True, stop=True)
                            last.then_inc(s_rows, 1)

                @block.gpsimd
                def _(pool):
                    def step(g):
                        for s in range(2):
                            n = 2 * g + s
                            pool.wait_ge(s_index, n + 1)
                            pool.wait_ge(s_done, n + 3)
                            for u in range(U):
                                wait_over(pool, s_added[s * U + u], 16 * g)
                                pool.nop(nofuse=True)
                                nc.gpsimd.indirect_dma_start(
                                    out=sums1[s * U + u][:, :], in_=sums[:, s, u, :], in_offset=None, compute_op=ALU.add,
                                    out_offset=bass.IndirectOffsetOnAxis(ap=index[:, s, u:u + 1], axis=0)).then_inc(s_added[s * U + u], 16)

                    peeled(pool, LOOP, step)
                    for k in range(2 * U):
                        pool.wait_ge(s_added[k], 16 * LOOP)

        with ExitStack() as st:
            sb, ps, sem = alloc(st)
            total = HN[:, 0:TN * W1].rearrange("p (t c) -> p t c", t=TN)
            part = [sb(f"part1_{i}", [P, TN, W1]) for i in range(2)]
            bias = sb("bias1", [P, 2, C])
            s_first, s_bias, s_chain, s_used = (sem(n + "_f1") for n in ("s_first", "s_bias", "s_chain", "s_used"))
            s_part = sem("s_part_f1", 2)
            with nc.Block() as block:
                @block.sync
                def _(sp):
                    sp.dma_start(total, sums1[0][0:TN * P, :].rearrange("(t p) c -> p t c", p=P)).then_inc(s_first, 16)
                    for i in range(2):
                        sp.dma_start(bias[:, i, :], a[f"L1_gnn_lin{i + 1}_b"].unsqueeze(0).to_broadcast([P, C])).then_inc(s_bias, 16)
                    for k in range(1, COPIES):
                        if k > 2:
                            sp.wait_ge(s_used, k - 2)
                        sp.dma_start(part[k % 2][:, :, :], sums1[k][0:TN * P, :].rearrange("(t p) c -> p t c", p=P)).then_inc(s_part[k % 2], 16)
                    sp.wait_ge(s_used, COPIES - 1)

                @block.vector
                def _(dve):
                    link = Chain(dve, s_chain)
                    dve.wait_ge(s_bias, 32)
                    link(nc.vector.tensor_tensor(LIN[:, :, 0:C], LIN[:, :, 0:C], bias[:, 0, :].unsqueeze(1).to_broadcast([P, TN, C]), ALU.add))
                    link(nc.vector.tensor_tensor(LIN[:, :, C:2 * C], LIN[:, :, C:2 * C], bias[:, 1, :].unsqueeze(1).to_broadcast([P, TN, C]), ALU.add))
                    link(nc.vector.tensor_tensor(X[:, :, :], X[:, :, :], LIN[:, :, C:2 * C], ALU.add))
                    dve.wait_ge(s_first, 16)
                    for k in range(1, COPIES):
                        dve.wait_ge(s_part[k % 2], 16 * ((k + 1) // 2))
                        nc.vector.tensor_tensor(total, total, part[k % 2][:, :, :], ALU.add).then_inc(s_used, 1)
                        dve.wait_ge(s_used, k)
                    link(nc.vector.tensor_tensor(X[:, :, :], X[:, :, :], total[:, :, 0:C], ALU.add))
                    link(nc.vector.tensor_tensor(LIN[:, :, 0:C], LIN[:, :, 0:C], total[:, :, C:W1].to_broadcast([P, TN, C]), ALU.mult))
                    link(nc.vector.tensor_tensor(X[:, :, :], X[:, :, :], LIN[:, :, 0:C], ALU.add))

        clear_semaphores()

        def load2(sp, WT, WX, s_w):
            sp.dma_start(WX[0:F, 0:F], a["L2_gnn_W_up0"]).then_inc(s_w, 16)
            for c in range(3):
                sp.dma_start(WX[F + c:C:3, F * (c + 1):F * (c + 2)], a["L2_gnn_W_up1"]).then_inc(s_w, 16)

        def prepare2(link, WT, WX):
            link(nc.vector.tensor_scalar(WT[:, :], WX[:, 0:C], float(F ** -0.5), None, ALU.mult))

        node_stage(2, C, table2, load2, 4, prepare2, clear=True)

        with ExitStack() as st:
            sb, ps, sem = alloc(st)
            unit = HN[:, 0:3 * T].rearrange("p (t c) -> p t c", c=3)
            square = sb("square2", [P, T])
            length = sb("length2", [P, T])
            w0 = sb("w0_2", [2 * NB, P])
            w1 = sb("w1_2", [P, P])
            w2 = sb("w2_2", [P, 2, P])
            b01 = sb("b01_2", [P, 2])
            b2 = sb("b2_2", [3, P])
            b2hi = sb("b2hi", [3, P], BF16)
            b2mid = sb("b2mid", [3, P], BF16)
            b2lo = sb("b2lo", [3, P], BF16)
            b2rest = sb("b2rest", [3, P])
            b2row = sb("b2row", [P, P], BF16)
            three = sb("three", [P, P], BF16)
            index = sb("index2", [P, 2, U], I32)
            rows = sb("rows2", [P, 2, U, C])
            base = sb("base2", [2 * NB, 2, 2 * P])
            h1 = sb("h1_2", [P, 2 * P])
            h2 = sb("h2_2", [P, 2, 2 * P])
            hot = sb("hot2", [P, 2, U, P])
            mid = sb("mid2", [P, 2, U, 2 * C])
            q1 = sb("q1_2", [P, U, F])
            dot = sb("dot2", [P, U, 3, F])
            psA = ps("psA2", [P, 2, 2 * P])
            psW = ps("psW2", [P, 2, U, P])
            psS = ps("psS2", [P, 4, 2, 2 * P])
            (s_in, s_chain, s_root, s_sq, s_begin, s_h0, s_h1, s_h1p, s_h2, s_hot, s_w, s_mid, s_sum, s_free, s_done, s_set) = (sem(n + "_e2") for n in (
                "s_in", "s_chain", "s_root", "s_sq", "s_begin", "s_h0", "s_h1", "s_h1p", "s_h2", "s_hot", "s_w", "s_mid", "s_sum", "s_free", "s_done", "s_set"))
            s_rows = gathered2
            s_index, s_base = (sem(n, 2) for n in ("s_index_e2", "s_base_e2"))
            with nc.Block() as block:
                @block.sync
                def _(sp):
                    sp.wait_ge(s_set, 1)
                    sp.dma_start(unit, a["vectors"]).then_inc(s_in, 16)
                    for i in range(2):
                        sp.dma_start(w0[i * NB:(i + 1) * NB, i * HID:(i + 1) * HID], a["L2_gnn_mlp_w0"]).then_inc(s_in, 16)
                        half = slice(i * HID, (i + 1) * HID)
                        sp.dma_start(w1[half, half], a["L2_gnn_mlp_w1"]).then_inc(s_in, 16)
                        sp.dma_start(w2[half, i, :], a["L2_gnn_mlp_w2"]).then_inc(s_in, 16)
                        sp.dma_start(b01[half, 0:1], a["L2_gnn_mlp_b0"].unsqueeze(1)).then_inc(s_in, 16)
                        sp.dma_start(b01[half, 1:2], a["L2_gnn_mlp_b1"].unsqueeze(1)).then_inc(s_in, 16)
                    sp.dma_start(b2[:, :], a["L2_gnn_mlp_b2"].unsqueeze(0).to_broadcast([3, P])).then_inc(s_in, 16)
                    sp.wait_ge(s_in, 16 * 12)
                    with sp.Fori(0, LOOP) as g:
                        for s in range(2):
                            n = 2 * g + s
                            sp.wait_ge(s_done, n + 1)
                            sp.dma_start(index[:, s, :], a["src_groups"][bass.ds(n, 1), :, :].rearrange("b p t -> (b p) t")).then_inc(s_index[s], 16)
                            sp.dma_start(base[:, s, :], basis.rearrange("g h i e -> (g h i) e")[bass.ds(n * 2 * NB, 2 * NB), :]).then_inc(s_base[s], 16)
                    for s in range(2):
                        sp.wait_ge(s_index[s], 16 * LOOP)
                        sp.wait_ge(s_base[s], 16 * LOOP)

                @block.gpsimd
                def _(pool):
                    with pool.Fori(0, LOOP) as g:
                        for s in range(2):
                            pool.wait_ge(s_index[s], 16 * g + 16)
                            pool.nop(nofuse=True)
                            for u in range(U):
                                nc.gpsimd.indirect_dma_start(
                                    out=rows[:, s, u, :], out_offset=None, in_=table2[:, :],
                                    in_offset=bass.IndirectOffsetOnAxis(ap=index[:, s, u:u + 1], axis=0)).then_inc(s_rows[s], 16)
                    for s in range(2):
                        pool.wait_ge(s_rows[s], 16 * U * LOOP)

                @block.scalar
                def _(act):
                    act.wait_ge(s_sq, 1)
                    nc.scalar.activation(length[:, :], square[:, :], ACT.Sqrt).then_inc(s_root, 1)
                    with act.Fori(0, LOOP) as g:
                        for s in range(2):
                            n = 2 * g + s
                            act.wait_ge(s_h0, n + 1)
                            nc.scalar.activation(h1[:, :], psA[:, 0, :], ACT.Silu, bias=b01[:, 0:1]).then_inc(s_h1, 1)
                            act.wait_ge(s_h1p, n + 1)
                            nc.scalar.activation(h2[:, s, :], psA[:, 1, :], ACT.Silu, bias=b01[:, 1:2]).then_inc(s_h2, 1)

                @block.vector
                def _(dve):
                    link = Chain(dve, s_chain)
                    link(nc.vector.memset(w0[:, :], 0.0))
                    link(nc.vector.memset(w1[:, :], 0.0))
                    link(nc.vector.memset(w2[:, :, :], 0.0))
                    dve.sem_inc(s_set, 1)
                    link(nc.vector.memset(ACC[:, :, :], 0.0))
                    link(nc.vector.memset(b2row[:, :], 0.0))
                    link(nc.vector.memset(three[:, :], 0.0))
                    dve.wait_ge(s_in, 16 * 12)
                    link(nc.vector.memset(three[0:3, :], 1.0))
                    link(nc.vector.tensor_copy(b2hi[:, :], b2[:, :]))
                    link(nc.vector.tensor_tensor(b2rest[:, :], b2[:, :], b2hi[:, :], ALU.subtract))
                    link(nc.vector.tensor_copy(b2mid[:, :], b2rest[:, :]))
                    link(nc.vector.tensor_tensor(b2rest[:, :], b2rest[:, :], b2mid[:, :], ALU.subtract))
                    link(nc.vector.tensor_copy(b2lo[:, :], b2rest[:, :]))
                    link(nc.vector.tensor_scalar(b2row[0:3, :], b2hi[:, :], K[0:3, 0:1], None, ALU.mult))
                    link(nc.vector.scalar_tensor_tensor(b2row[0:3, :], b2mid[:, :], K[0:3, 1:2], b2row[0:3, :], ALU.mult, ALU.add))
                    link(nc.vector.scalar_tensor_tensor(b2row[0:3, :], b2lo[:, :], K[0:3, 2:3], b2row[0:3, :], ALU.mult, ALU.add))
                    link(nc.vector.tensor_tensor(square[:, :], unit[:, :, 0], unit[:, :, 0], ALU.mult))
                    for c in range(1, 3):
                        link(nc.vector.tensor_tensor(length[:, :], unit[:, :, c], unit[:, :, c], ALU.mult))
                        link(nc.vector.tensor_tensor(square[:, :], square[:, :], length[:, :], ALU.add))
                    dve.sem_inc(s_sq, 1)
                    dve.wait_ge(s_root, 1)
                    link(nc.vector.tensor_scalar(length[:, :], length[:, :], 1e-12, None, ALU.add))
                    link(nc.vector.reciprocal(length[:, :], length[:, :]))
                    link(nc.vector.tensor_tensor(unit, unit, length[:, :].unsqueeze(2).to_broadcast([P, T, 3]), ALU.mult))
                    dve.sem_inc(s_done, 2)
                    dve.sem_inc(s_free, 4)
                    with dve.Fori(0, LOOP) as g:
                        link.loop(g, 2 * (5 + U))
                        for s in range(2):
                            n = 2 * g + s
                            one_hots(hot[:, s, :, :], n).then_inc(s_hot, 1)
                            dve.wait_ge(s_rows[s], 16 * U * g + 16 * U)
                            dve.wait_ge(s_w, n + 1)
                            scalars = rows[:, s, :, 0:F]
                            vectors = rows[:, s, :, F:C].rearrange("p u (c k) -> p u c k", c=3)
                            along = unit[:, bass.ds(n * U, U), :].unsqueeze(3).to_broadcast([P, U, 3, F])
                            m1 = mid[:, s, :, 2 * F:5 * F].rearrange("p u (c k) -> p u c k", c=3)
                            m2 = mid[:, s, :, 5 * F:8 * F].rearrange("p u (c k) -> p u c k", c=3)
                            weights = [psW[:, s, :, i * F:(i + 1) * F] for i in range(4)]
                            link(nc.vector.tensor_tensor(dot[:, :, :, :], vectors, along, ALU.mult))
                            nc.vector.tensor_tensor(mid[:, s, :, 0:F], weights[0], scalars, ALU.mult)
                            link(nc.vector.tensor_tensor(q1[:, :, :], weights[1], scalars, ALU.mult))
                            nc.vector.tensor_tensor(m1, q1[:, :, :].unsqueeze(2).to_broadcast([P, U, 3, F]), along, ALU.mult)
                            nc.vector.tensor_tensor(m2, weights[2].unsqueeze(2).to_broadcast([P, U, 3, F]), vectors, ALU.mult)
                            link(nc.vector.tensor_tensor(dot[:, :, 0, :], dot[:, :, 0, :], dot[:, :, 1, :], ALU.add))
                            link(nc.vector.tensor_tensor(dot[:, :, 0, :], dot[:, :, 0, :], dot[:, :, 2, :], ALU.add))
                            link(nc.vector.tensor_tensor(mid[:, s, :, F:2 * F], weights[3], dot[:, :, 0, :], ALU.mult))
                            dve.sem_inc(s_mid, 1)
                            dve.sem_inc(s_done, 1)
                            for u in range(U):
                                first = window(dve, n * U + u)
                                dve.wait_ge(s_sum, n * U + (u + 1))
                                link(nc.vector.tensor_tensor(ACC[:, :, bass.ds(first, P)], ACC[:, :, bass.ds(first, P)], psS[:, u, :, 0:P], ALU.add))
                                dve.sem_inc(s_free, 1)
                    link.end(LOOP)

                @block.tensor
                def _(pe):
                    with pe.Fori(0, LOOP) as g:
                        for s in range(2):
                            n = 2 * g + s
                            pe.wait_ge(s_base[s], 16 * g + 16)
                            nc.tensor.matmul(psA[:, 0, :], w0[:, :], base[:, s, :], start=True, stop=True).then_inc(s_h0, 1)
                            pe.wait_ge(s_h1, n + 1)
                            nc.tensor.matmul(psA[:, 1, :], w1[:, :], h1[:, :], start=True, stop=True).then_inc(s_h1p, 1)
                            pe.wait_ge(s_h2, n + 1)
                            pe.wait_ge(s_done, n + 1)
                            for u in range(U):
                                nc.tensor.matmul(psW[:, s, u, :], h2[:, s, (u % 2) * P:(u % 2 + 1) * P], w2[:, u // 2, :], start=True, stop=False)
                                last = nc.tensor.matmul(psW[:, s, u, :], three[:, :], b2row[:, :], start=False, stop=True)
                            last.then_inc(s_w, 1)
                            pe.wait_ge(s_hot, n + 1)
                            pe.wait_ge(s_mid, n + 1)
                            for u in range(U):
                                pe.wait_ge(s_free, n * U + (u + 1))
                                for b in range(2):
                                    last = nc.tensor.matmul(psS[:, u, b, 0:P], mid[:, s, u, b * C:(b + 1) * C], hot[:, s, u, :], start=True, stop=True)
                                last.then_inc(s_sum, 1)

        def finish(L, load, n_load, prepare):
            with ExitStack() as st:
                sb, ps, sem = alloc(st)
                WA = sb(f"WA{L}", [P, 2, C])
                stage = sb(f"stage{L}", [P, TG * C])
                psP = ps(f"psP{L}", [P, 2, 512])
                psT = ps(f"psT_f{L}", [P, 8, C])
                s_in, s_ready, s_chain, s_proj, s_stage, s_turn, s_added = (sem(f"{n}_f{L}") for n in (
                    "s_in", "s_ready", "s_chain", "s_proj", "s_stage", "s_turn", "s_added"))
                with nc.Block() as block:
                    @block.sync
                    def _(sp):
                        load(sp, WA, s_in)
                        sp.wait_ge(s_in, 16 * n_load)

                    @block.vector
                    def _(dve):
                        link = Chain(dve, s_chain)
                        dve.wait_ge(s_in, 16 * n_load)
                        prepare(link, WA)
                        dve.sem_inc(s_ready, 1)
                        with dve.Fori(0, TN // TG) as g:
                            dve.wait_ge(s_turn, g + 1)
                            at = X[:, bass.ds(g * TG, TG), :]
                            nc.vector.tensor_tensor(at, at, psT[:, 0:TG, :], ALU.add).then_inc(s_added, 1)

                    @block.scalar
                    def _(act):
                        with act.Fori(0, TN // TG) as g:
                            act.wait_ge(s_proj, g + 1)
                            nc.scalar.copy(stage[:, :].rearrange("p (b e) -> p b e", b=2), psP[:, :, 0:TG * C // 2]).then_inc(s_stage, 1)

                    @block.tensor
                    def _(pe):
                        pe.wait_ge(s_ready, 1)
                        with pe.Fori(0, TN // TG) as g:
                            for b in range(2):
                                cols = bass.ds(g * (TG * C) + b * (TG * C // 2), TG * C // 2)
                                nc.tensor.matmul(psP[:, b, 0:TG * C // 2], WA[:, 0, :], ACC[:, 0, cols], start=True, stop=False)
                                last = nc.tensor.matmul(psP[:, b, 0:TG * C // 2], WA[:, 1, :], ACC[:, 1, cols], start=False, stop=True)
                            last.then_inc(s_proj, 1)
                            pe.wait_ge(s_stage, g + 1)
                            for i in range(TG):
                                last = nc.tensor.transpose(psT[:, i, :], stage[:, i * C:(i + 1) * C], ident)
                            last.then_inc(s_turn, 1)
                            pe.wait_ge(s_added, g + 1)

        with ExitStack() as st:
            sb, ps, sem = alloc(st)
            wst = sb("wst2", [P, 2, F])

            def load_out(sp, WA, s_in):
                sp.dma_start(wst[0:2 * F, 0, :], a["L2_gnn_W_out0"]).then_inc(s_in, 16)
                for part in range(2):
                    for c in range(3):
                        block, at = divmod(2 + 3 * part + c, 4)
                        sp.dma_start(wst[at * F:(at + 1) * F, block, :], a["L2_gnn_W_out1"][part * F:(part + 1) * F, :]).then_inc(s_in, 16)

            def prepare_out(link, WA):
                scale = 1.0 / ((2 * F) ** 0.5 * 16.0)
                link(nc.vector.memset(WA[:, :, :], 0.0))
                link(nc.vector.tensor_scalar(WA[0:2 * F, 0, 0:F], wst[0:2 * F, 0, :], scale, None, ALU.mult))
                for part in range(2):
                    for c in range(3):
                        block, at = divmod(2 + 3 * part + c, 4)
                        own = slice(at * F, (at + 1) * F)
                        link(nc.vector.tensor_scalar(WA[own, block, F + c:C:3], wst[own, block, :],
                                                     scale * (3.0 ** 0.5 if part == 0 else 1.0), None, ALU.mult))

            finish(2, load_out, 7, prepare_out)

        clear_semaphores()

        node_stage(3, C, table3, lambda sp, WT, WX, s_w: sp.dma_start(WT[:, :], a["L3_gnn_W"]).then_inc(s_w, 16), 1,
                   lambda link, WT, WX: None, scale=DINV)

        with ExitStack() as st:
            sb, ps, sem = alloc(st)
            R = 4
            last = EDGE_GROUPS - 1
            index = sb("index3", [P, R, U], I32)
            rows = sb("rows3", [P, R, U, C])
            hot = sb("hot3", [P, 2, U, P])
            psS = ps("psS3", [P, 4, 512])
            s_chain, s_hot, s_sum, s_free, s_done = (sem(n + "_e3") for n in ("s_chain", "s_hot", "s_sum", "s_free", "s_done"))
            s_rows = gathered3
            s_index = sem("s_index_e3", R)
            with nc.Block() as block:
                @block.sync
                def _(sp):
                    def load(n, g, r):
                        sp.wait_ge(s_done, n + 1)
                        sp.dma_start(index[:, r, :], a["src_groups"][bass.ds(n, 1), :, :].rearrange("b p t -> (b p) t")).then_inc(s_index[r], 16)

                    ring(sp, EDGE_GROUPS, R, load)
                    for r in range(R):
                        sp.wait_ge(s_index[r], 16 * uses(EDGE_GROUPS, R, r))

                @block.gpsimd
                def _(pool):
                    def gather(n, g, r):
                        pool.wait_ge(s_index[r], 16 * g + 16)
                        pool.nop(nofuse=True)
                        for u in range(U):
                            nc.gpsimd.indirect_dma_start(
                                out=rows[:, r, u, :], out_offset=None, in_=table3[:, :],
                                in_offset=bass.IndirectOffsetOnAxis(ap=index[:, r, u:u + 1], axis=0)).then_inc(s_rows[r], 16)

                    ring(pool, EDGE_GROUPS, R, gather)
                    for r in range(R):
                        pool.wait_ge(s_rows[r], 16 * U * uses(EDGE_GROUPS, R, r))

                @block.vector
                def _(dve):
                    link = Chain(dve, s_chain)
                    link(nc.vector.memset(ACC[:, 0, :], 0.0))
                    dve.sem_inc(s_done, R)
                    dve.sem_inc(s_free, 4)
                    one_hots(hot[:, 0, :, :], 0).then_inc(s_hot, 1)

                    def add(n, g, r):
                        if not (isinstance(n, int) and n == last):
                            one_hots(hot[:, (r + 1) % 2, :, :], n + 1).then_inc(s_hot, 1)
                        for u in range(U):
                            first = window(dve, n * U + u)
                            dve.wait_ge(s_sum, n * U + (u + 1))
                            own = ACC[:, 0, bass.ds(first, P)]
                            nc.vector.tensor_tensor(own, own, psS[:, u, 0:P], ALU.add).then_inc(s_free, 1)
                            dve.wait_ge(s_free, n * U + (u + 5))
                        dve.sem_inc(s_done, 1)

                    ring(dve, EDGE_GROUPS, R, add)

                @block.tensor
                def _(pe):
                    def sums(n, g, r):
                        pe.wait_ge(s_hot, n + 1)
                        pe.wait_ge(s_rows[r], 16 * U * g + 16 * U)
                        for u in range(U):
                            pe.wait_ge(s_free, n * U + (u + 1))
                            nc.tensor.matmul(psS[:, u, 0:P], rows[:, r, u, :], hot[:, r % 2, u, :], start=True, stop=True).then_inc(s_sum, 1)

                    ring(pe, EDGE_GROUPS, R, sums)

        with ExitStack() as st:
            sb, ps, sem = alloc(st)
            own = sb("own3", [P, TN, C])
            AGG = ACC[:, 1, 0:TN * C].rearrange("p (t c) -> p t c", t=TN)
            hn = HN[:, 0:TN * C].rearrange("p (t c) -> p t c", t=TN)
            rowsB = sb("rowsB3", [P, 3, C])
            mean = sb("mean_f3", [P, TN])
            var = sb("var_f3", [P, TN])
            stage = sb("stage3", [P, TG * C])
            psT = ps("psT_f3", [P, 8, C])
            s_in, s_chain, s_stage, s_turn, s_added, s_var, s_sqrt = (sem(n + "_f3") for n in (
                "s_in", "s_chain", "s_stage", "s_turn", "s_added", "s_var", "s_sqrt"))
            with nc.Block() as block:
                @block.sync
                def _(sp):
                    sp.dma_start(own[:, :, :], table3[0:TN * P, :].rearrange("(t p) c -> p t c", p=P)).then_inc(s_in, 16)
                    for i, name in enumerate(("bias", "ln_gamma", "ln_beta")):
                        sp.dma_start(rowsB[:, i, :], a["L3_gnn_" + name].unsqueeze(0).to_broadcast([P, C])).then_inc(s_in, 16)
                    sp.wait_ge(s_in, 64)

                @block.scalar
                def _(act):
                    with act.Fori(0, TN // TG) as g:
                        nc.scalar.copy(stage[:, :], ACC[:, 0, bass.ds(g * TG * C, TG * C)]).then_inc(s_stage, 1)
                        act.wait_ge(s_turn, g + 1)
                    act.wait_ge(s_var, 1)
                    nc.scalar.activation(var[:, :], var[:, :], ACT.Sqrt).then_inc(s_sqrt, 1)

                @block.tensor
                def _(pe):
                    with pe.Fori(0, TN // TG) as g:
                        pe.wait_ge(s_stage, g + 1)
                        for i in range(TG):
                            done = nc.tensor.transpose(psT[:, i, :], stage[:, i * C:(i + 1) * C], ident)
                        done.then_inc(s_turn, 1)
                        pe.wait_ge(s_added, g + 1)

                @block.vector
                def _(dve):
                    link = Chain(dve, s_chain)
                    link(nc.vector.scalar_tensor_tensor(X[:, :, :], hn, 0.0, X[:, :, :], ALU.max, ALU.add))
                    dve.wait_ge(s_in, 64)
                    with dve.Fori(0, TN // TG) as g:
                        dve.wait_ge(s_turn, g + 1)
                        nc.vector.tensor_tensor(AGG[:, bass.ds(g * TG, TG), :], own[:, bass.ds(g * TG, TG), :], psT[:, 0:TG, :], ALU.add).then_inc(s_added, 1)
                    dve.wait_ge(s_added, TN // TG)

                    def per_node(v):
                        return v.unsqueeze(2).to_broadcast([P, TN, C])

                    def per_channel(i):
                        return rowsB[:, i, :].unsqueeze(1).to_broadcast([P, TN, C])

                    link(nc.vector.tensor_tensor(AGG, AGG, per_node(DINV[:, :]), ALU.mult))
                    link(nc.vector.tensor_tensor(AGG, AGG, per_channel(0), ALU.add))
                    link(nc.vector.reduce_sum(mean[:, :], AGG, axis=AX))
                    link(nc.vector.tensor_scalar(mean[:, :], mean[:, :], 1.0 / C, None, ALU.mult))
                    link(nc.vector.tensor_tensor(AGG, AGG, per_node(mean[:, :]), ALU.subtract))
                    link(nc.vector.tensor_tensor(own[:, :, :], AGG, AGG, ALU.mult))
                    link(nc.vector.reduce_sum(var[:, :], own[:, :, :], axis=AX))
                    nc.vector.tensor_scalar(var[:, :], var[:, :], 1.0 / C, EPS, ALU.mult, ALU.add).then_inc(s_var, 1)
                    dve.wait_ge(s_sqrt, 1)
                    link(nc.vector.reciprocal(var[:, :], var[:, :]))
                    link(nc.vector.tensor_tensor(AGG, AGG, per_node(var[:, :]), ALU.mult))
                    link(nc.vector.tensor_tensor(AGG, AGG, per_channel(1), ALU.mult))
                    link(nc.vector.tensor_tensor(AGG, AGG, per_channel(2), ALU.add))
                    link(nc.vector.tensor_scalar(AGG, AGG, 0.0, None, ALU.max))
                    link(nc.vector.tensor_tensor(X[:, :, :], X[:, :, :], AGG, ALU.add))

        with ExitStack() as st:
            _, _, sem = alloc(st)
            s_res = sem("s_res")
            with nc.Block() as block:
                @block.sync
                def _(sp):
                    sp.dma_start(out[0:(TN - 1) * P, :].rearrange("(t p) c -> p t c", p=P), X[:, 0:TN - 1, :]).then_inc(s_res, 16)
                    sp.dma_start(out[(TN - 1) * P:N, :], X[0:N - (TN - 1) * P, TN - 1, :]).then_inc(s_res, 16)
                    sp.wait_ge(s_res, 32)


_OUT = ((N, C), "float32")


def kernel(**inputs):
    import concourse.bacc as bacc
    from concourse.bass_utils import run_bass_kernel_spmd as run

    nc = bacc.Bacc("TRN2", target_bir_lowering=False, num_devices=1)
    pad = T * P - E
    src = np.pad(np.asarray(inputs["src"]), (0, pad)).reshape(T, P)
    dst = np.pad(np.asarray(inputs["dst"]), (0, pad), constant_values=N).reshape(T, P)
    weight = np.pad(np.asarray(inputs["edge_weight"]), (0, pad)).reshape(T, P)
    vectors = np.pad(np.asarray(inputs["edge_attr_3"]), ((0, pad), (0, 0)), constant_values=1.0).reshape(T, P, 3)
    arrays = {
        "consts": constants(), "x": inputs["x"],
        "src_rows": src, "dst_rows": dst, "weight_rows": weight,
        "src_cols": src.T, "dst_cols": dst.T, "weight_cols": weight.T,
        "dst_first": dst[None, :, 0], "dst_last": dst[None, :, P - 1],
        "src_groups": src.reshape(T // U, U, P).transpose(0, 2, 1),
        "src_batches": src.reshape(T // B0, B0, P).transpose(0, 2, 1),
        "vectors": vectors.transpose(1, 0, 2),
        "L1_gnn_lin1_w": np.asarray(inputs["L1_gnn_lin1_w"]).T, "L1_gnn_lin2_w": np.asarray(inputs["L1_gnn_lin2_w"]).T,
    }
    for name in inputs:
        if name.startswith("L") and name not in arrays:
            arrays[name] = inputs[name]
    arrays = {"in_" + k: np.ascontiguousarray(v) for k, v in arrays.items()}
    a = {k[3:]: nc.dram_tensor(k, v.shape, mybir.dt.from_np(v.dtype), kind="ExternalInput").ap() for k, v in arrays.items()}
    out = nc.dram_tensor("out", _OUT[0], F32, kind="ExternalOutput").ap()
    build(nc, a, out)
    r = run(nc, [arrays], core_ids=[0])
    return r.results[0]["out"]
```

```python
import concourse.bass as bass
from concourse import mybir
from contextlib import ExitStack
import numpy as np

F32, BF16, I32 = mybir.dt.float32, mybir.dt.bfloat16, mybir.dt.int32
ALU = mybir.AluOpType
ACT = mybir.ActivationFunctionType
AX = mybir.AxisListType.X

P = 128
N = 6250
E = 206250
C = 128
H, F = 4, 32
NB = 8
HID = 64
TN = (N + P - 1) // P
NPAD = (TN + 1) * P
TG = 7
U = 4
B0 = 16
T = 102 * B0
GROUPS = T // U
EDGE_GROUPS = -(-E // (P * U))
LOOP = -(-E // (P * U * 2))
BATCHES = -(-E // (P * B0))
W0 = 2 * H + C
W1 = C + 1
COPIES = 2 * U
BIG = 1e30
EPS = 1e-5
CI, CJ, CT, CH, CM, CP, CR, CO, CEND = 0, 128, 256, 384, 512, 528, 529, 530, 658
RQ = 12
RG = GROUPS // RQ
RH = RG // 2


def constants():
    k = np.zeros((P, CEND), np.float32)
    k[:, CI:CJ] = np.eye(P)
    k[:, CJ:CT] = np.arange(P)[None, :]
    k[:, CT:CH] = np.arange(P)[None, :] < np.arange(P)[:, None]
    rows = np.arange(H * B0)
    k[:H * B0, CH:CM] = (rows[:, None] // B0) == (np.arange(P)[None, :] // F)
    k[:H * B0, CM:CP] = (rows[:, None] % B0) == np.arange(B0)[None, :]
    k[:, CP] = TN * P + np.arange(P)
    k[:NB * RQ, CR] = -(np.arange(NB * RQ) // RQ)
    k[0:3, CO:CEND] = 1.0
    return k


class Chain:

    def __init__(self, eng, sem):
        self.eng, self.sem, self.done, self.step, self.per = eng, sem, 0, None, 0

    def loop(self, step, per):
        self.step, self.per, self.n = step, per, 0

    def end(self, times):
        assert self.n == self.per, (self.n, self.per)
        self.done += times * self.per
        self.step = None

    def __call__(self, ins):
        ins.then_inc(self.sem, 1)
        if self.step is None:
            self.done += 1
            self.eng.wait_ge(self.sem, self.done)
        else:
            self.n += 1
            self.eng.wait_ge(self.sem, self.step * self.per + (self.done + self.n))


def wait_over(eng, sem, value):
    if not isinstance(value, int) or value > 0:
        eng.wait_ge(sem, value)


def ring(eng, total, slots, step):
    with eng.Fori(0, total // slots) as g:
        for r in range(slots):
            step(slots * g + r, g, r)
    for n in range(total - total % slots, total):
        step(n, n // slots, n % slots)


def peeled_ring(eng, total, slots, step):
    for n in range(slots):
        step(n, 0, n)
    with eng.Fori(1, total // slots) as g:
        for r in range(slots):
            step(slots * g + r, g, r)
    for n in range(total - total % slots, total):
        step(n, n // slots, n % slots)


def uses(total, slots, r):
    return (total - r + slots - 1) // slots


def build(nc, a, out):
    ctx = ExitStack()

    def dram(name, shape, dt=F32):
        return nc.dram_tensor(name, shape, dt, kind="Internal").ap()

    table0 = dram("table0", [NPAD, W0])
    table1 = dram("table1", [NPAD, W1])
    table2 = dram("table2", [NPAD, C])
    table3 = dram("table3", [NPAD, C])
    sums1 = [dram(f"sums1_{i}", [NPAD, W1]) for i in range(COPIES)]
    src_f = dram("src_f", [T, P])
    dst_f = dram("dst_f", [T, P])
    basis = dram("basis", [GROUPS, 2, NB, 2 * P])
    count_d = dram("count_d", [NPAD])

    used_sems = []

    with ctx:
        def clear_semaphores():
            with nc.Block() as block:
                @block.gpsimd
                def _(pool):
                    for each in used_sems:
                        pool.sem_clear(each)
            used_sems.clear()

        def alloc(stack):
            def sb(name, shape, dt=F32):
                return stack.enter_context(nc.sbuf_tensor(name, shape, dt))

            def ps(name, shape, dt=F32):
                return stack.enter_context(nc.psum_tensor(name, shape, dt))

            def one_sem(name):
                used_sems.append(stack.enter_context(nc.semaphore(name)))
                return used_sems[-1]

            def sem(name, n=None):
                return one_sem(name) if n is None else [one_sem(f"{name}{i}") for i in range(n)]
            return sb, ps, sem

        sb, _, _ = alloc(ctx)

        def pool_sems(name, n):
            return [ctx.enter_context(nc.semaphore(f"{name}{i}")) for i in range(n)]

        gathered0, scattered1 = pool_sems("gathered0_", 4), pool_sems("scattered1_", 2 * U)
        gathered2, gathered3 = pool_sems("gathered2_", 4), pool_sems("gathered3_", 4)
        K = sb("K", [P, CEND])
        X = sb("X", [P, TN, C])
        HN = sb("HN", [P, NPAD])
        ACC = sb("ACC", [P, 2, NPAD])
        SRC = sb("SRC", [P, T])
        REL = sb("REL", [P, T])
        DINV = sb("DINV", [P, TN])
        D0 = sb("D0", [1, T], I32)
        ident = K[:, CI:CJ]
        lane = K[:, CJ:CT]

        def nodes(table, width):
            return table[0:TN * P, :].rearrange("(t p) c -> p t c", p=P)[:, :, 0:width]

        def one_hots(dst, n):
            return nc.vector.tensor_tensor(
                dst, lane.unsqueeze(1).to_broadcast([P, dst.shape[1], P]),
                REL[:, bass.ds(n * dst.shape[1], dst.shape[1])].unsqueeze(2).to_broadcast([P, dst.shape[1], P]),
                ALU.is_equal)

        def windows(eng, tile):
            _, firsts = nc.values_load_multi_w_load_instructions(
                D0[0:1, bass.ds(tile, U)], engines=(eng.engine,), min_val=0, max_val=N,
                skip_runtime_bounds_check_because="a dst is a node number, and padding edges end at N")
            return firsts

        def flat(ap):
            return ap.rearrange("t e -> (t e)").rearrange("(p k) -> p k", p=P)

        with ExitStack() as st:
            sb, ps, sem = alloc(st)
            dst_i = sb("dst_i", [P, T], I32)
            src_i = sb("src_i", [P, T], I32)
            dcol_i = sb("dcol_i", [P, T], I32)
            scol_i = sb("scol_i", [P, T], I32)
            first_i = sb("first_i", [P, T], I32)
            radius = ACC[0:NB * RQ, :, :].rearrange("p b n -> p (b n)")[:, 0:RH * U * P]
            cutoff = sb("cutoff", [NB * RQ, RH * U * P])
            dst_v, src_v, first_v = HN[:, 0:T], HN[:, T:2 * T], HN[:, 2 * T:3 * T]
            s_in, s_x, s_pad, s_float, s_out, s_chain, s_len, s_clip, s_exp, s_act, s_basis, s_stored = (sem(n) for n in (
                "s_in", "s_x", "s_pad", "s_float", "s_out", "s_chain", "s_len", "s_clip", "s_exp", "s_act", "s_basis", "s_stored"))
            with nc.Block() as block:
                @block.sync
                def _(sp):
                    sp.dma_start(K[:, :], a["consts"]).then_inc(s_in, 16)
                    sp.dma_start(dst_i[:, :], flat(a["dst_rows"])).then_inc(s_in, 16)
                    sp.dma_start(src_i[:, :], flat(a["src_rows"])).then_inc(s_in, 16)
                    sp.dma_start(dcol_i[:, :], a["dst_cols"]).then_inc(s_in, 16)
                    sp.dma_start(scol_i[:, :], a["src_cols"]).then_inc(s_in, 16)
                    sp.dma_start(first_i[:, :], a["dst_first"].to_broadcast([P, T])).then_inc(s_in, 16)
                    sp.dma_start(D0[:, :], a["dst_first"]).then_inc(s_in, 16)
                    sp.dma_start(X[:, 0:TN - 1, :], a["x"][0:(TN - 1) * P, :].rearrange("(t p) c -> p t c", p=P)).then_inc(s_x, 16)
                    sp.wait_ge(s_pad, 1)
                    sp.dma_start(X[0:N - (TN - 1) * P, TN - 1, :], a["x"][(TN - 1) * P:N, :]).then_inc(s_x, 16)
                    sp.wait_ge(s_float, 2)
                    sp.dma_start(flat(dst_f), dst_v).then_inc(s_out, 16)
                    sp.dma_start(flat(src_f), src_v).then_inc(s_out, 16)
                    sp.wait_ge(s_out, 32)
                    sp.wait_ge(s_x, 32)

                @block.scalar
                def _(act):
                    lengths = a["weight_rows"].rearrange("t e -> (t e)").rearrange("(q k) -> q k", q=RQ)
                    groups = basis.rearrange("(q f g) h i e -> q f g h i e", q=RQ, f=2)
                    for half in range(2):
                        if half:
                            act.wait_ge(s_stored, 16 * 2 * NB)
                        for i in range(NB):
                            act.dma_start(radius[i * RQ:(i + 1) * RQ, :],
                                          lengths[:, half * RH * U * P:(half + 1) * RH * U * P]).then_inc(s_len, 16)
                        act.wait_ge(s_in, 16 * 7)
                        act.wait_ge(s_clip, half + 1)
                        nc.scalar.activation(radius, radius, ACT.Square, bias=K[0:NB * RQ, CR:CR + 1],
                                             scale=float(NB - 1)).then_inc(s_act, 1)
                        act.wait_ge(s_act, half + 1)
                        nc.scalar.activation(radius, radius, ACT.Exp, scale=-0.5).then_inc(s_exp, 1)
                        act.wait_ge(s_basis, half + 1)
                        for i in range(NB):
                            for h in range(2):
                                act.dma_start(
                                    groups[:, half, :, h, i, :],
                                    radius[i * RQ:(i + 1) * RQ, :].rearrange("q (g h e) -> q g h e", g=RH, h=2)[:, :, h, :]
                                ).then_inc(s_stored, 16)
                    act.wait_ge(s_stored, 16 * 2 * 2 * NB)

                @block.vector
                def _(dve):
                    link = Chain(dve, s_chain)
                    nc.vector.memset(X[:, TN - 1, :], 0.0).then_inc(s_pad, 1)
                    dve.wait_ge(s_in, 16 * 7)
                    nc.vector.tensor_copy(dst_v, dst_i[:, :]).then_inc(s_float, 1)
                    nc.vector.tensor_copy(src_v, src_i[:, :]).then_inc(s_float, 1)
                    nc.vector.tensor_copy(SRC[:, :], scol_i[:, :])
                    nc.vector.tensor_copy(REL[:, :], dcol_i[:, :])
                    link(nc.vector.tensor_copy(first_v, first_i[:, :]))
                    link(nc.vector.tensor_tensor(REL[:, :], REL[:, :], first_v, ALU.subtract))
                    for half in range(2):
                        dve.wait_ge(s_len, 16 * NB * (half + 1))
                        link(nc.vector.tensor_scalar(cutoff[:, :], radius, 1.0, float(NB ** 0.5), ALU.is_le, ALU.mult))
                        nc.vector.tensor_scalar(radius, radius, 0.0, 1.0, ALU.max, ALU.min).then_inc(s_clip, 1)
                        dve.wait_ge(s_exp, half + 1)
                        nc.vector.tensor_tensor(radius, radius, cutoff[:, :], ALU.mult).then_inc(s_basis, 1)

        def node_stage(L, width, table, load, n_load, prepare, ones=0, extra=None, scale=None, clear=False):
            with ExitStack() as st:
                sb, ps, sem = alloc(st)
                hn = HN[:, 0:TN * C].rearrange("p (t c) -> p t c", t=TN)
                TAB = sb(f"TAB{L}", [P, TN, width + ones])
                sq = TAB[:, :, 0:C]
                WT = sb(f"WT{L}", [P, width])
                WX = sb(f"WX{L}", [P, 2 * C])
                mean = sb(f"mean{L}", [P, TN])
                var = sb(f"var{L}", [P, TN])
                turn = sb(f"turn{L}", [P, TG, C])
                turned = sb(f"turned{L}", [P, TG, C])
                psT = ps(f"psT{L}", [P, 8, C])
                psM = ps(f"psM{L}", [P, 8, 2 * C])
                s_w, s_chain, s_var, s_sqrt, s_rows, s_t, s_ht, s_prod, s_tab, s_done, s_ones, s_out = (sem(f"{n}_{L}") for n in (
                    "s_w", "s_chain", "s_var", "s_sqrt", "s_rows", "s_t", "s_ht", "s_prod", "s_tab", "s_done", "s_ones", "s_out"))
                s_clear = sem(f"s_clear_{L}")
                steps = TN // TG
                with nc.Block() as block:
                    @block.sync
                    def _(sp):
                        if clear:
                            sp.wait_ge(s_clear, 1)
                        load(sp, WT, WX, s_w)
                        sp.wait_ge(s_w, 16 * n_load)
                        sp.wait_ge(s_done, steps)
                        if ones:
                            sp.wait_ge(s_ones, 1)
                        sp.dma_start(table[0:TN * P, :].rearrange("(t p) c -> p t c", p=P), TAB[:, :, :]).then_inc(s_out, 16)
                        sp.dma_start(table[TN * P:NPAD, :], TAB[:, 0, :]).then_inc(s_out, 16)
                        sp.wait_ge(s_out, 32)

                    @block.vector
                    def _(dve):
                        link = Chain(dve, s_chain)
                        if clear:
                            nc.vector.memset(WX[:, :], 0.0).then_inc(s_clear, 1)
                        dve.wait_ge(s_w, 16 * n_load)
                        prepare(link, WT, WX)
                        link(nc.vector.reduce_sum(mean[:, :], X[:, :, :], axis=AX))
                        link(nc.vector.tensor_scalar(mean[:, :], mean[:, :], 1.0 / C, None, ALU.mult))
                        link(nc.vector.tensor_tensor(hn, X[:, :, :], mean[:, :].unsqueeze(2).to_broadcast([P, TN, C]), ALU.subtract))
                        link(nc.vector.tensor_tensor(sq, hn, hn, ALU.mult))
                        link(nc.vector.reduce_sum(var[:, :], sq, axis=AX))
                        nc.vector.tensor_scalar(var[:, :], var[:, :], 1.0 / C, EPS, ALU.mult, ALU.add).then_inc(s_var, 1)
                        dve.wait_ge(s_sqrt, 1)
                        link(nc.vector.reciprocal(var[:, :], var[:, :]))
                        link(nc.vector.tensor_tensor(hn, hn, var[:, :].unsqueeze(2).to_broadcast([P, TN, C]), ALU.mult))
                        if ones:
                            nc.vector.memset(TAB[:, :, width:width + ones], 1.0).then_inc(s_ones, 1)
                        nc.vector.tensor_scalar(turn[:, :, :], hn[:, 0:TG, :], 0.0, None, ALU.max).then_inc(s_rows, 1)

                        def store(at):
                            if extra is not None:
                                nc.vector.tensor_copy(extra[:, at, 0:C], psM[:, 0:TG, C:2 * C])
                                nc.vector.tensor_copy(extra[:, at, C:2 * C], psT[:, 0:TG, :])
                            if scale is None:
                                nc.vector.tensor_copy(TAB[:, at, 0:width], psM[:, 0:TG, 0:width]).then_inc(s_done, 1)
                            else:
                                nc.vector.tensor_tensor(TAB[:, at, 0:width], psM[:, 0:TG, 0:width],
                                                        scale[:, at].unsqueeze(2).to_broadcast([P, TG, width]), ALU.mult).then_inc(s_done, 1)

                        with dve.Fori(0, steps - 1) as g:
                            dve.wait_ge(s_t, g + 1)
                            nc.vector.tensor_scalar(turn[:, :, :], hn[:, bass.ds((g + 1) * TG, TG), :], 0.0, None, ALU.max).then_inc(s_rows, 1)
                            dve.wait_ge(s_prod, g + 1)
                            store(bass.ds(g * TG, TG))
                        dve.wait_ge(s_prod, steps)
                        store(slice((steps - 1) * TG, TN))

                    @block.scalar
                    def _(act):
                        act.wait_ge(s_var, 1)
                        nc.scalar.activation(var[:, :], var[:, :], ACT.Sqrt).then_inc(s_sqrt, 1)
                        with act.Fori(0, steps) as g:
                            act.wait_ge(s_t, g + 1)
                            nc.scalar.copy(turned[:, :, :], psT[:, 0:TG, :]).then_inc(s_ht, 1)

                    @block.tensor
                    def _(pe):
                        with pe.Fori(0, steps) as g:
                            pe.wait_ge(s_rows, g + 1)
                            for i in range(TG):
                                last = nc.tensor.transpose(psT[:, i, :], turn[:, i, :], ident)
                            last.then_inc(s_t, 1)
                            pe.wait_ge(s_ht, g + 1)
                            for i in range(TG):
                                if extra is None:
                                    last = nc.tensor.matmul(psM[:, i, 0:width], turned[:, i, :], WT[:, :], start=True, stop=True)
                                else:
                                    nc.tensor.matmul(psM[:, i, 0:C], turned[:, i, :], WT[:, :], start=True, stop=True)
                                    nc.tensor.matmul(psM[:, i, C:2 * C], turned[:, i, :], WX[:, 0:C], start=True, stop=True)
                                    last = nc.tensor.matmul(psT[:, i, :], turned[:, i, :], WX[:, C:2 * C], start=True, stop=True)
                            last.then_inc(s_prod, 1)
                            pe.wait_ge(s_done, g + 1)

        def load0(sp, WT, WX, s_w):
            sp.dma_start(WT[:, 0:C], a["L0_gnn_W"]).then_inc(s_w, 16)
            for i, name in enumerate(("L0_gnn_attn_l", "L0_gnn_attn_r")):
                row = a[name].rearrange("h f -> (h f)").unsqueeze(0)
                sp.dma_start(WX[:, i * C:(i + 1) * C], row.to_broadcast([P, C])).then_inc(s_w, 16)

        def prepare0(link, WT, WX):
            for i in range(2):
                part = WX[:, i * C:(i + 1) * C]
                link(nc.vector.tensor_tensor(part, WT[:, 0:C], part, ALU.mult))
                link(nc.vector.reduce_sum(WT[:, C + i * H:C + (i + 1) * H], part.rearrange("p (h f) -> p h f", h=H), axis=AX))

        node_stage(0, W0, table0, load0, 3, prepare0)

        with ExitStack() as st:
            sb, ps, sem = alloc(st)
            R0 = H * B0
            CNT = HN[0:1, :]
            R = 4
            last = BATCHES - 1
            index = sb("index0", [P, R, B0], I32)
            rows = sb("rows0", [P, R, B0, W0])
            er = sb("er0", [P, R, B0, H])
            hot = sb("hot0", [P, 2, B0, P])
            hotT = sb("hotT0", [P, 2, 4, P])
            drow = sb("drow0", [R0, R, P])
            cut = sb("cut0", [R0, P + 1])
            score = sb("score0", [P, H, B0])
            scoreR = sb("scoreR0", [R0, P])
            low = sb("low0", [R0, P])
            top = sb("top0", [R0, P])
            shifted = sb("shifted0", [R0, P + 1])
            carryC = sb("carryC0", [R0, 1])
            tail = sb("tail0", [1, R0])
            run = sb("run0", [1, H, B0 + 1])
            carry = sb("carry0", [1, H, B0])
            prob = sb("prob0", [P, 2, B0, H, F])
            fadeL = sb("fadeL0", [R0, P])
            fade = sb("fade0", [P, 2, B0])
            sameR = sb("sameR", [1, T], BF16)
            sameC = sb("sameC", [1, T], BF16)
            lasts = rows[0:1, :, :, :].rearrange("o s t c -> o (s t c)").bitcast(I32)[:, 0:T]
            first_f = hot[0:1, 0, :, :].rearrange("o t e -> o (t e)")[:, 0:T]
            last_f = hot[0:1, 1, :, :].rearrange("o t e -> o (t e)")[:, 0:T]
            zero = sb("zero", [P, W1])
            one_col = sb("one_col", [P, 1])
            psH = ps("psH0", [P, 2, 4, P])
            psE = ps("psE0", [P, 512])
            psS = ps("psS0", [R0, 512])
            psB = ps("psB0", [P, 512])
            psA = ps("psA0", [P, 2, 4, P])
            names = ("s_last", "s_ready", "s_hot", "s_turn", "s_hotT", "s_er", "s_score", "s_scoreR", "s_low", "s_tail",
                     "s_carry", "s_carryC", "s_shift", "s_exp", "s_probR", "s_fadeL", "s_fade", "s_msg", "s_sum", "s_free",
                     "s_batch", "s_chain", "s_out")
            s_count, s_prob, s_zero, s_clear = (sem(n + "_e0") for n in ("s_count", "s_prob", "s_zero", "s_clear"))
            (s_last, s_ready, s_hot, s_turn, s_hotT, s_er, s_score, s_scoreR, s_low, s_tail, s_carry, s_carryC, s_shift,
             s_exp, s_probR, s_fadeL, s_fade, s_msg, s_sum, s_free, s_batch, s_chain, s_out) = (sem(n + "_e0") for n in names)
            s_rows = gathered0
            s_index, s_erw, s_drow = (sem(n, R) for n in ("s_index_e0", "s_erw_e0", "s_drow_e0"))
            with nc.Block() as block:
                @block.sync
                def _(sp):
                    sp.dma_start(lasts, a["dst_last"]).then_inc(s_last, 16)

                    def load(n, g, r):
                        sp.wait_ge(s_batch, n + 1)
                        sp.dma_start(index[:, r, :], a["src_batches"][bass.ds(n, 1), :, :].rearrange("b p t -> (b p) t")).then_inc(s_index[r], 16)
                        for h in range(H):
                            sp.dma_start(drow[h * B0:(h + 1) * B0, r, :], dst_f[bass.ds(n * B0, B0), :]).then_inc(s_drow[r], 16)
                        for k in range(B0):
                            if k % U == 0:
                                firsts = windows(sp, n * B0 + k)
                            sp.dma_start(er[:, r, k, :], table0[bass.ds(firsts[k % U], P), C + H:C + 2 * H]).then_inc(s_erw[r], 16)

                    ring(sp, BATCHES, R, load)
                    for r in range(R):
                        sp.wait_ge(s_index[r], 16 * uses(BATCHES, R, r))
                        sp.wait_ge(s_drow[r], 16 * H * uses(BATCHES, R, r))
                        sp.wait_ge(s_erw[r], 16 * B0 * uses(BATCHES, R, r))
                    sp.wait_ge(s_batch, R + BATCHES)
                    sp.dma_start(count_d.unsqueeze(0), CNT[:, :]).then_inc(s_out, 16)
                    sp.wait_ge(s_out, 16)

                @block.gpsimd
                def _(pool):
                    def gather(n, g, r):
                        pool.wait_ge(s_index[r], 16 * g + 16)
                        pool.nop(nofuse=True)
                        for k in range(B0):
                            nc.gpsimd.indirect_dma_start(
                                out=rows[:, r, k, :], out_offset=None, in_=table0[:, :],
                                in_offset=bass.IndirectOffsetOnAxis(ap=index[:, r, k:k + 1], axis=0)).then_inc(s_rows[r], 16)

                    ring(pool, BATCHES, R, gather)
                    for r in range(R):
                        pool.wait_ge(s_rows[r], 16 * B0 * uses(BATCHES, R, r))

                @block.scalar
                def _(act):
                    act.wait_ge(s_zero, 1)
                    for k in range(COPIES):
                        act.dma_start(sums1[k].rearrange("(t p) c -> p t c", p=P), zero[:, :].unsqueeze(1).to_broadcast([P, NPAD // P, W1])).then_inc(s_clear, 16)

                    def step(n, g, r):
                        for q in range(B0 // 4):
                            act.wait_ge(s_turn, n * (B0 // 4) + (q + 1))
                            nc.scalar.copy(hotT[:, q % 2, :, :], psH[:, q % 2, :, :]).then_inc(s_hotT, 1)
                        act.wait_ge(s_shift, n + 1)
                        nc.scalar.activation(shifted[:, :], shifted[:, :], ACT.Exp).then_inc(s_exp, 1)
                        act.wait_ge(s_probR, n + 1)
                        act.wait_ge(s_batch, n + (R - 1))
                        nc.scalar.copy(prob[:, r % 2, :, :, :], psB[:, 128:128 + R0].rearrange("p (h t) -> p t h", h=H).unsqueeze(3).to_broadcast([P, B0, H, F])).then_inc(s_prob, 1)

                    ring(act, BATCHES, R, step)
                    act.wait_ge(s_clear, 16 * COPIES)

                @block.vector
                def _(dve):
                    link = Chain(dve, s_chain)
                    dve.wait_ge(s_last, 16)
                    link(nc.vector.memset(ACC[:, :, :], 0.0))
                    nc.vector.memset(CNT[:, :], 0.0)
                    nc.vector.memset(one_col[:, :], 1.0)
                    nc.vector.memset(zero[:, :], 0.0).then_inc(s_zero, 1)
                    nc.vector.memset(cut[:, :], 0.0)
                    link(nc.vector.memset(run[:, :, :], -BIG))
                    nc.vector.tensor_copy(first_f, D0[:, :])
                    link(nc.vector.tensor_copy(last_f, lasts))
                    link(nc.vector.memset(sameR[:, :], 1.0))
                    link(nc.vector.memset(sameC[:, :], 1.0))
                    link(nc.vector.tensor_tensor(sameR[:, 1:T], last_f[:, 1:T], last_f[:, 0:T - 1], ALU.not_equal))
                    link(nc.vector.tensor_tensor(sameC[:, 1:T], first_f[:, 1:T], last_f[:, 0:T - 1], ALU.not_equal))
                    link(nc.vector.tensor_scalar(sameR[:, :], sameR[:, :], -BIG, None, ALU.mult))
                    link(nc.vector.tensor_scalar(sameC[:, :], sameC[:, :], -BIG, None, ALU.mult))
                    dve.sem_inc(s_batch, R)
                    dve.sem_inc(s_count, 1)
                    dve.sem_inc(s_free, 2)
                    dve.sem_inc(s_ready, 1)

                    def front(n, g, r, between=lambda first, end: None):
                        s = r % 2
                        one_hots(hot[:, s, :, :], n).then_inc(s_hot, 1)
                        dve.wait_ge(s_drow[r], 16 * H * g + 16 * H)
                        link(nc.vector.tensor_tensor(cut[:, 1:P], drow[:, r, 1:P], drow[:, r, 0:P - 1], ALU.not_equal))
                        link(nc.vector.tensor_scalar(cut[:, 1:P], cut[:, 1:P], -BIG, None, ALU.mult))
                        between(0, 8)
                        dve.wait_ge(s_er, n + 1)
                        dve.wait_ge(s_rows[r], 16 * B0 * g + 16 * B0)
                        link(nc.vector.tensor_tensor(score[:, :, :], rows[:, r, :, C:C + H].rearrange("p t h -> p h t"),
                                                     psE[:, 0:R0].rearrange("p (t h) -> p h t", t=B0), ALU.add))
                        nc.vector.scalar_tensor_tensor(score[:, :, :], score[:, :, :], 0.2, score[:, :, :], ALU.mult, ALU.max).then_inc(s_score, 1)
                        between(8, 10)
                        dve.wait_ge(s_scoreR, n + 1)
                        link(nc.vector.tensor_copy(scoreR[:, :], psS[:, 0:P]))
                        nc.vector.tensor_tensor_scan(low[:, :], cut[:, 0:P], scoreR[:, :], -BIG, ALU.add, ALU.max).then_inc(s_low, 1)
                        between(10, 11)
                        dve.wait_ge(s_tail, n + 1)
                        link(nc.vector.tensor_copy(tail[:, :], psB[0:1, 0:R0]))
                        for h in range(H):
                            scan = nc.vector.tensor_tensor_scan(run[:, h, 1:B0 + 1], sameR[:, bass.ds(n * B0, B0)], tail[:, h * B0:(h + 1) * B0],
                                                                run[:, h, 0:1], ALU.add, ALU.max)
                        link(scan)
                        nc.vector.tensor_tensor(carry[:, :, :], run[:, :, 0:B0], sameC[:, bass.ds(n * B0, B0)].unsqueeze(1).to_broadcast([1, H, B0]), ALU.add).then_inc(s_carry, 1)
                        dve.wait_ge(s_carry, n + 1)
                        link(nc.vector.tensor_copy(run[:, :, 0:1], run[:, :, B0:B0 + 1]))
                        between(11, 12)
                        dve.wait_ge(s_carryC, n + 1)
                        link(nc.vector.tensor_copy(carryC[:, :], psS[:, 256:257]))
                        link(nc.vector.tensor_tensor_scan(low[:, :], cut[:, 0:P], scoreR[:, :], carryC[:, :], ALU.add, ALU.max))
                        link(nc.vector.tensor_tensor_scan(top[:, ::-1], cut[:, P:0:-1], low[:, ::-1], -BIG, ALU.add, ALU.max))
                        nc.vector.tensor_tensor(shifted[:, P:P + 1], carryC[:, :], top[:, 0:1], ALU.subtract)
                        nc.vector.tensor_tensor(shifted[:, 0:P], scoreR[:, :], top[:, :], ALU.subtract).then_inc(s_shift, 1)
                        between(12, 14)
                        dve.wait_ge(s_exp, n + 1)
                        nc.vector.tensor_scalar(fadeL[:, :], K[0:R0, CH:CM], shifted[:, P:P + 1], None, ALU.mult).then_inc(s_fadeL, 1)
                        between(14, 16)
                        dve.wait_ge(s_fade, n + 1)
                        link(nc.vector.tensor_copy(fade[:, s, :], psE[:, 256:256 + B0]))
                        dve.wait_ge(s_prob, n + 1)
                        nc.vector.tensor_tensor(rows[:, r, :, 0:C], rows[:, r, :, 0:C], prob[:, s, :, :, :].rearrange("p t h f -> p t (h f)"),
                                                ALU.mult).then_inc(s_msg, 1)

                    def add(n, s, firsts, first, end):
                        for k in range(first, end):
                            at = firsts[k]
                            dve.wait_ge(s_sum, n * B0 + (k + 1))
                            dve.wait_ge(s_count, n * B0 + (k + 1))
                            count = CNT[:, bass.ds(at, P)]
                            nc.vector.tensor_tensor(count, count, psA[0:1, k % 2, 2, :], ALU.add).then_inc(s_count, 1)
                            dve.wait_ge(s_free, n * B0 + (k + 2))
                            node = ACC[:, :, bass.ds(at, 1)]
                            nc.vector.scalar_tensor_tensor(node, node, fade[:, s, k:k + 1], psA[:, k % 2, 0:2, 0:1], ALU.mult, ALU.add)
                            others = ACC[:, :, bass.ds(at + 1, P - 1)]
                            nc.vector.tensor_tensor(others, others, psA[:, k % 2, 0:2, 1:P], ALU.add).then_inc(s_free, 1)

                    def step(n, g, r):
                        firsts = []
                        for k in range(0, B0, U):
                            firsts += windows(dve, n * B0 + k)
                        if isinstance(n, int) and n == last:
                            add(n, r % 2, firsts, 0, B0)
                        else:
                            front(n + 1, g if r < R - 1 else g + 1, (r + 1) % R, lambda first, end: add(n, r % 2, firsts, first, end))
                        dve.wait_ge(s_free, (n + 1) * B0 + 2)
                        dve.sem_inc(s_batch, 1)

                    front_links = 11
                    link.loop(0, front_links)
                    front(0, 0, 0)
                    link.end(1)
                    with dve.Fori(0, BATCHES // R) as g:
                        link.loop(g, R * front_links)
                        for r in range(R):
                            step(R * g + r, g, r)
                    link.end(BATCHES // R)
                    step(last, last // R, last % R)

                @block.tensor
                def _(pe):
                    pe.wait_ge(s_ready, 1)

                    def front(n, g, r, between=lambda first, end: None):
                        s = r % 2
                        pe.wait_ge(s_hot, n + 1)
                        pe.wait_ge(s_erw[r], 16 * B0 * g + 16 * B0)
                        for q in range(B0 // 4 + 1):
                            if q < B0 // 4:
                                for k in range(4):
                                    done = nc.tensor.transpose(psH[:, q % 2, k, :], hot[:, s, 4 * q + k, :], ident)
                                done.then_inc(s_turn, 1)
                            if q < B0 // 4:
                                between(2 * q, 2 * q + 2)
                            if q > 0:
                                pe.wait_ge(s_hotT, n * (B0 // 4) + q)
                                for k in range(4 * q - 4, 4 * q):
                                    done = nc.tensor.matmul(psE[:, k * H:(k + 1) * H], hotT[:, (q - 1) % 2, k % 4, :], er[:, r, k, :], start=True, stop=True)
                        done.then_inc(s_er, 1)
                        between(8, 10)
                        pe.wait_ge(s_score, n + 1)
                        pe.nop(nofuse=True)
                        nc.tensor.transpose(psS[:, 0:P], score[:, :, :].rearrange("p h t -> p (h t)"), ident).then_inc(s_scoreR, 1)
                        between(10, 11)
                        pe.wait_ge(s_low, n + 1)
                        pe.nop(nofuse=True)
                        nc.tensor.transpose(psB[0:1, 0:R0], low[:, P - 1:P], ident[0:R0, 0:R0]).then_inc(s_tail, 1)
                        between(11, 12)
                        pe.wait_ge(s_carry, n + 1)
                        pe.nop(nofuse=True)
                        nc.tensor.transpose(psS[:, 256:257], carry[:, :, :].rearrange("o h t -> o (h t)"), ident[0:1, 0:1]).then_inc(s_carryC, 1)
                        between(12, 14)
                        pe.wait_ge(s_exp, n + 1)
                        pe.nop(nofuse=True)
                        nc.tensor.transpose(psB[:, 128:128 + R0], shifted[:, 0:P], ident[0:R0, 0:R0]).then_inc(s_probR, 1)
                        pe.wait_ge(s_fadeL, n + 1)
                        nc.tensor.matmul(psE[:, 256:256 + B0], fadeL[:, :], K[0:R0, CM:CP], start=True, stop=True).then_inc(s_fade, 1)
                        between(14, 16)

                    def sums(n, r, first, end):
                        if first == 0:
                            pe.wait_ge(s_msg, n + 1)
                        for k in range(first, end):
                            pe.wait_ge(s_free, n * B0 + (k + 1))
                            nc.tensor.matmul(psA[:, k % 2, 0, :], rows[:, r, k, 0:C], hot[:, r % 2, k, :], start=True, stop=True)
                            nc.tensor.matmul(psA[:, k % 2, 1, :], prob[:, r % 2, k, :, :].rearrange("p h f -> p (h f)"), hot[:, r % 2, k, :], start=True, stop=True)
                            nc.tensor.matmul(psA[0:1, k % 2, 2, :], one_col[:, :], hot[:, r % 2, k, :], start=True, stop=True).then_inc(s_sum, 1)

                    def step(n, g, r):
                        if isinstance(n, int) and n == last:
                            sums(n, r, 0, B0)
                        else:
                            front(n + 1, g if r < R - 1 else g + 1, (r + 1) % R, lambda first, end: sums(n, r, first, end))

                    front(0, 0, 0)
                    ring(pe, BATCHES, R, step)

        with ExitStack() as st:
            sb, ps, sem = alloc(st)
            wo = sb("wo", [P, C])
            cols = sb("cols0", [P, 4])
            degree = sb("degree", [P, TN])
            stat = sb("stat0", [P, 4])
            stage = sb("stage0", [P, TG * C])
            psP = ps("psP0", [P, 2, 512])
            psT = ps("psT_f0", [P, 8, C])
            (s_in, s_chain, s_rst, s_proj, s_o, s_free, s_var, s_sqrt, s_deg, s_root, s_stage, s_turn, s_added) = (sem(n + "_f0") for n in (
                "s_in", "s_chain", "s_rst", "s_proj", "s_o", "s_free", "s_var", "s_sqrt", "s_deg", "s_root", "s_stage", "s_turn", "s_added"))
            CH0 = 400
            with nc.Block() as block:
                @block.sync
                def _(sp):
                    sp.dma_start(wo[:, :], a["L0_gnn_Wo"]).then_inc(s_in, 16)
                    for i, name in enumerate(("bias", "bo", "gamma", "beta")):
                        sp.dma_start(cols[:, i:i + 1], a["L0_gnn_" + name].unsqueeze(1)).then_inc(s_in, 16)
                    sp.dma_start(degree[:, :], count_d[0:TN * P].rearrange("(t p) -> p t", p=P), allow_slow_non_contiguous=True).then_inc(s_in, 16)
                    sp.wait_ge(s_in, 16 * 6)

                @block.vector
                def _(dve):
                    link = Chain(dve, s_chain)
                    sums, total = ACC[:, 0, :], ACC[:, 1, :]
                    link(nc.vector.tensor_scalar(total, total, 1e-30, None, ALU.max))
                    link(nc.vector.reciprocal(total, total))
                    link(nc.vector.tensor_tensor(sums, sums, total, ALU.mult))
                    dve.wait_ge(s_in, 16 * 6)
                    nc.vector.tensor_scalar(sums, sums, cols[:, 0:1], None, ALU.add).then_inc(s_rst, 1)
                    nc.vector.tensor_scalar(degree[:, :], degree[:, :], 1.0, None, ALU.add).then_inc(s_deg, 1)
                    with dve.Fori(0, NPAD // CH0 // 2) as g:
                        for s in range(2):
                            dve.wait_ge(s_proj, 2 * g + (s + 1))
                            nc.vector.tensor_scalar(HN[:, bass.ds((2 * g + s) * CH0, CH0)], psP[:, s, 0:CH0], cols[:, 1:2], None, ALU.add).then_inc(s_o, 1)
                    dve.wait_ge(s_o, NPAD // CH0)
                    o = HN[:, 0:N]
                    link(nc.vector.reduce_sum(stat[:, 0:1], o, axis=AX))
                    link(nc.vector.tensor_scalar(stat[:, 0:1], stat[:, 0:1], 1.0 / N, None, ALU.mult))
                    link(nc.vector.tensor_scalar(HN[:, :], HN[:, :], stat[:, 0:1], None, ALU.subtract))
                    link(nc.vector.tensor_tensor(total[:, 0:N], o, o, ALU.mult))
                    link(nc.vector.reduce_sum(stat[:, 1:2], total[:, 0:N], axis=AX))
                    nc.vector.tensor_scalar(stat[:, 1:2], stat[:, 1:2], 1.0 / N, EPS, ALU.mult, ALU.add).then_inc(s_var, 1)
                    dve.wait_ge(s_sqrt, 1)
                    nc.vector.reciprocal(DINV[:, :], degree[:, :])
                    link(nc.vector.reciprocal(stat[:, 1:2], stat[:, 1:2]))
                    link(nc.vector.tensor_tensor(stat[:, 2:3], stat[:, 1:2], cols[:, 2:3], ALU.mult))
                    dve.sem_inc(s_root, 1)
                    with dve.Fori(0, TN // TG) as g:
                        dve.wait_ge(s_turn, g + 1)
                        nc.vector.tensor_tensor(X[:, bass.ds(g * TG, TG), :], X[:, bass.ds(g * TG, TG), :], psT[:, 0:TG, :], ALU.add).then_inc(s_added, 1)

                @block.scalar
                def _(act):
                    act.wait_ge(s_deg, 1)
                    nc.scalar.activation(degree[:, :], degree[:, :], ACT.Sqrt)
                    act.wait_ge(s_var, 1)
                    nc.scalar.activation(stat[:, 1:2], stat[:, 1:2], ACT.Sqrt).then_inc(s_sqrt, 1)
                    act.wait_ge(s_root, 1)
                    with act.Fori(0, TN // TG) as g:
                        nc.scalar.activation(stage[:, :], HN[:, bass.ds(g * TG * C, TG * C)], ACT.Identity, bias=cols[:, 3:4], scale=stat[:, 2:3]).then_inc(s_stage, 1)
                        act.wait_ge(s_turn, g + 1)

                @block.tensor
                def _(pe):
                    pe.wait_ge(s_rst, 1)
                    with pe.Fori(0, NPAD // CH0 // 2) as g:
                        for s in range(2):
                            nc.tensor.matmul(psP[:, s, 0:CH0], wo[:, :], ACC[:, 0, bass.ds((2 * g + s) * CH0, CH0)], start=True, stop=True).then_inc(s_proj, 1)
                        pe.wait_ge(s_o, 2 * g + 2)
                    with pe.Fori(0, TN // TG) as g:
                        pe.wait_ge(s_stage, g + 1)
                        for i in range(TG):
                            last = nc.tensor.transpose(psT[:, i, :], stage[:, i * C:(i + 1) * C], ident)
                        last.then_inc(s_turn, 1)
                        pe.wait_ge(s_added, g + 1)

        clear_semaphores()

        LIN = ACC[:, :, :].rearrange("p b n -> p (b n)")[:, 0:TN * 2 * C].rearrange("p (t c) -> p t c", t=TN)

        def load1(sp, WT, WX, s_w):
            sp.dma_start(WT[:, :], a["L1_gnn_weight"]).then_inc(s_w, 16)
            sp.dma_start(WX[:, 0:C], a["L1_gnn_lin1_w"]).then_inc(s_w, 16)
            sp.dma_start(WX[:, C:2 * C], a["L1_gnn_lin2_w"]).then_inc(s_w, 16)

        node_stage(1, C, table1, load1, 3, lambda link, WT, WX: None, ones=1, extra=LIN)

        with ExitStack() as st:
            sb, ps, sem = alloc(st)
            R = 4
            weight = sb("weight1", [P, T])
            dst_i = sb("dst_i1", [P, T], I32)
            other = sb("other1", [P, T])
            srow = sb("srow1", [P, R, U, P])
            win = sb("win1", [P, R, U, W1])
            same = sb("same1", [P, 2, U, P])
            hotW = sb("hotW1", [P, 2, U, P])
            mix = sb("mix1", [P, 2, U, P])
            before = sb("before1", [P, U, P])
            later = sb("later1", [P, U])
            place = sb("place1", [P, U])
            index = sb("index1", [P, 2, U], I32)
            sums = sb("sumrows1", [P, 2, U, W1])
            psX = ps("psX1", [P, 2, U, P])
            psV = ps("psV1", [P, 2, U, 2 * P])
            (s_in, s_chain, s_same, s_hot, s_mix, s_mixed, s_rows, s_index, s_done) = (sem(n + "_e1") for n in (
                "s_in", "s_chain", "s_same", "s_hot", "s_mix", "s_mixed", "s_rows", "s_index", "s_done"))
            s_srow, s_win = (sem(n, R) for n in ("s_srow_e1", "s_win_e1"))
            s_added = scattered1
            with nc.Block() as block:
                @block.sync
                def _(sp):
                    sp.dma_start(weight[:, :], a["weight_cols"]).then_inc(s_in, 16)
                    sp.dma_start(dst_i[:, :], a["dst_cols"]).then_inc(s_in, 16)

                    def load(n, g, r):
                        sp.wait_ge(s_done, n + 1)
                        sp.dma_start(srow[:, r, :, :].rearrange("p u e -> p (u e)"), src_f[bass.ds(n * U, U), :].rearrange("t e -> (t e)").unsqueeze(0).to_broadcast([P, U * P])).then_inc(s_srow[r], 16)
                        firsts = windows(sp, n * U)
                        for u in range(U):
                            sp.dma_start(win[:, r, u, :], table1[bass.ds(firsts[u], P), :]).then_inc(s_win[r], 16)

                    ring(sp, EDGE_GROUPS, R, load)
                    for r in range(R):
                        sp.wait_ge(s_srow[r], 16 * uses(EDGE_GROUPS, R, r))
                        sp.wait_ge(s_win[r], 16 * U * uses(EDGE_GROUPS, R, r))

                @block.vector
                def _(dve):
                    link = Chain(dve, s_chain)
                    dve.wait_ge(s_in, 32)
                    link(nc.vector.tensor_copy(other[:, :], dst_i[:, :]))
                    link(nc.vector.tensor_tensor(other[:, :], SRC[:, :], other[:, :], ALU.not_equal))
                    link(nc.vector.tensor_tensor(weight[:, :], weight[:, :], other[:, :], ALU.mult))

                    def step(n, g, r):
                        s = r % 2
                        dve.wait_ge(s_srow[r], 16 * g + 16)
                        wait_over(dve, s_mix, n - 1)
                        tile_src = SRC[:, bass.ds(n * U, U)]
                        nc.vector.tensor_tensor(same[:, s, :, :], srow[:, r, :, :], tile_src.unsqueeze(2).to_broadcast([P, U, P]), ALU.is_equal).then_inc(s_same, 1)
                        for u in range(U):
                            last = nc.vector.tensor_scalar(hotW[:, s, u, :], lane, REL[:, bass.ds(n * U + u, 1)],
                                                           weight[:, bass.ds(n * U + u, 1)], ALU.is_equal, ALU.mult)
                        last.then_inc(s_hot, 1)
                        dve.wait_ge(s_same, n + 1)
                        link(nc.vector.tensor_tensor(before[:, :, :], same[:, s, :, :], K[:, CT:CH].unsqueeze(1).to_broadcast([P, U, P]), ALU.mult))
                        link(nc.vector.reduce_max(later[:, :], before[:, :, :], axis=AX))
                        link(nc.vector.tensor_scalar(place[:, :], tile_src, -1.0, K[:, CP:CP + 1], ALU.mult, ALU.add))
                        link(nc.vector.tensor_tensor(place[:, :], place[:, :], later[:, :], ALU.mult))
                        link(nc.vector.tensor_tensor(place[:, :], place[:, :], tile_src, ALU.add))
                        for u in range(U):
                            wait_over(dve, s_added[s * U + u], 32 * g + 16 * (r // 2))
                        nc.vector.tensor_copy(index[:, s, :], place[:, :]).then_inc(s_index, 1)
                        dve.wait_ge(s_index, n + 1)

                    links = 5
                    link.loop(0, R * links)
                    for r in range(R):
                        step(r, 0, r)
                    link.end(1)
                    with dve.Fori(1, EDGE_GROUPS // R) as g:
                        link.loop(g - 1, R * links)
                        for r in range(R):
                            step(R * g + r, g, r)
                    link.end(EDGE_GROUPS // R - 1)
                    for n in range(EDGE_GROUPS // R * R, EDGE_GROUPS):
                        step(n, n // R, n % R)

                @block.scalar
                def _(act):
                    act.sem_inc(s_done, R)

                    def step(n, g, r):
                            s = r % 2
                            act.wait_ge(s_mix, n + 1)
                            nc.scalar.copy(mix[:, s, :, :], psX[:, s, :, :]).then_inc(s_mixed, 1)
                            act.wait_ge(s_rows, n + 1)
                            for u in range(U):
                                wait_over(act, s_added[s * U + u], 32 * g + 16 * (r // 2))
                            nc.scalar.copy(sums[:, s, :, :], psV[:, s, :, 0:W1]).then_inc(s_done, 1)

                    peeled_ring(act, EDGE_GROUPS, R, step)

                @block.tensor
                def _(pe):
                    def step(n, g, r):
                            s = r % 2
                            pe.wait_ge(s_hot, n + 1)
                            pe.wait_ge(s_same, n + 1)
                            for u in range(U):
                                last = nc.tensor.matmul(psX[:, s, u, :], hotW[:, s, u, :], same[:, s, u, :], start=True, stop=True)
                            last.then_inc(s_mix, 1)
                            pe.wait_ge(s_win[r], 16 * U * g + 16 * U)
                            pe.wait_ge(s_mixed, n + 1)
                            pe.wait_ge(s_done, n + (R - 1))
                            for u in range(U):
                                last = nc.tensor.matmul(psV[:, s, u, 0:W1], mix[:, s, u, :], win[:, r, u, :], start=True, stop=True)
                            last.then_inc(s_rows, 1)

                    ring(pe, EDGE_GROUPS, R, step)

                @block.gpsimd
                def _(pool):
                    def step(n, g, r):
                            s = r % 2
                            pool.wait_ge(s_index, n + 1)
                            pool.wait_ge(s_done, n + (R + 1))
                            for u in range(U):
                                wait_over(pool, s_added[s * U + u], 32 * g + 16 * (r // 2))
                                pool.nop(nofuse=True)
                                nc.gpsimd.indirect_dma_start(
                                    out=sums1[s * U + u][:, :], in_=sums[:, s, u, :], in_offset=None, compute_op=ALU.add,
                                    out_offset=bass.IndirectOffsetOnAxis(ap=index[:, s, u:u + 1], axis=0)).then_inc(s_added[s * U + u], 16)

                    peeled_ring(pool, EDGE_GROUPS, R, step)
                    for k in range(2 * U):
                        pool.wait_ge(s_added[k], 16 * uses(EDGE_GROUPS, 2, k // U))

        with ExitStack() as st:
            sb, ps, sem = alloc(st)
            total = HN[:, 0:TN * W1].rearrange("p (t c) -> p t c", t=TN)
            part = [sb(f"part1_{i}", [P, TN, W1]) for i in range(2)]
            bias = sb("bias1", [P, 2, C])
            s_first, s_bias, s_chain, s_used = (sem(n + "_f1") for n in ("s_first", "s_bias", "s_chain", "s_used"))
            s_part = sem("s_part_f1", 2)
            with nc.Block() as block:
                @block.sync
                def _(sp):
                    sp.dma_start(total, sums1[0][0:TN * P, :].rearrange("(t p) c -> p t c", p=P)).then_inc(s_first, 16)
                    for i in range(2):
                        sp.dma_start(bias[:, i, :], a[f"L1_gnn_lin{i + 1}_b"].unsqueeze(0).to_broadcast([P, C])).then_inc(s_bias, 16)
                    for k in range(1, COPIES):
                        if k > 2:
                            sp.wait_ge(s_used, k - 2)
                        sp.dma_start(part[k % 2][:, :, :], sums1[k][0:TN * P, :].rearrange("(t p) c -> p t c", p=P)).then_inc(s_part[k % 2], 16)
                    sp.wait_ge(s_used, COPIES - 1)

                @block.vector
                def _(dve):
                    link = Chain(dve, s_chain)
                    dve.wait_ge(s_bias, 32)
                    link(nc.vector.tensor_tensor(LIN[:, :, 0:C], LIN[:, :, 0:C], bias[:, 0, :].unsqueeze(1).to_broadcast([P, TN, C]), ALU.add))
                    link(nc.vector.tensor_tensor(LIN[:, :, C:2 * C], LIN[:, :, C:2 * C], bias[:, 1, :].unsqueeze(1).to_broadcast([P, TN, C]), ALU.add))
                    link(nc.vector.tensor_tensor(X[:, :, :], X[:, :, :], LIN[:, :, C:2 * C], ALU.add))
                    dve.wait_ge(s_first, 16)
                    for k in range(1, COPIES):
                        dve.wait_ge(s_part[k % 2], 16 * ((k + 1) // 2))
                        nc.vector.tensor_tensor(total, total, part[k % 2][:, :, :], ALU.add).then_inc(s_used, 1)
                        dve.wait_ge(s_used, k)
                    link(nc.vector.tensor_tensor(X[:, :, :], X[:, :, :], total[:, :, 0:C], ALU.add))
                    link(nc.vector.tensor_tensor(LIN[:, :, 0:C], LIN[:, :, 0:C], total[:, :, C:W1].to_broadcast([P, TN, C]), ALU.mult))
                    link(nc.vector.tensor_tensor(X[:, :, :], X[:, :, :], LIN[:, :, 0:C], ALU.add))

        clear_semaphores()

        def load2(sp, WT, WX, s_w):
            sp.dma_start(WX[0:F, 0:F], a["L2_gnn_W_up0"]).then_inc(s_w, 16)
            for c in range(3):
                sp.dma_start(WX[F + c:C:3, F * (c + 1):F * (c + 2)], a["L2_gnn_W_up1"]).then_inc(s_w, 16)

        def prepare2(link, WT, WX):
            link(nc.vector.tensor_scalar(WT[:, :], WX[:, 0:C], float(F ** -0.5), None, ALU.mult))

        node_stage(2, C, table2, load2, 4, prepare2, clear=True)

        with ExitStack() as st:
            sb, ps, sem = alloc(st)
            unit = HN[:, 0:3 * T].rearrange("p (t c) -> p t c", c=3)
            square = sb("square2", [P, T])
            length = sb("length2", [P, T])
            w0 = sb("w0_2", [2 * NB, P])
            w1 = sb("w1_2", [P, P])
            w2 = sb("w2_2", [P, 2, P])
            b01 = sb("b01_2", [P, 2])
            b2 = sb("b2_2", [3, P])
            b2hi = sb("b2hi", [3, P], BF16)
            b2mid = sb("b2mid", [3, P], BF16)
            b2lo = sb("b2lo", [3, P], BF16)
            b2rest = sb("b2rest", [3, P])
            b2row = sb("b2row", [P, P], BF16)
            three = sb("three", [P, P], BF16)
            R = 4
            last = EDGE_GROUPS - 1
            index = sb("index2", [P, R, U], I32)
            rows = sb("rows2", [P, R, U, C])
            base = sb("base2", [2 * NB, R, 2 * P])
            h1 = sb("h1_2", [P, 2 * P])
            h2 = sb("h2_2", [P, 2, 2 * P])
            hot = sb("hot2", [P, 2, U, P])
            mid = sb("mid2", [P, 2, U, 2 * C])
            q1 = sb("q1_2", [P, U, F])
            dot = sb("dot2", [P, U, 3, F])
            psA = ps("psA2", [P, 2, 2 * P])
            psW = ps("psW2", [P, 2, U, P])
            psS = ps("psS2", [P, 4, 2, 2 * P])
            (s_in, s_chain, s_root, s_sq, s_begin, s_h0, s_h1, s_h1p, s_h2, s_hot, s_w, s_mid, s_sum, s_free, s_dot, s_dot3, s_q1, s_set) = (sem(n + "_e2") for n in (
                "s_in", "s_chain", "s_root", "s_sq", "s_begin", "s_h0", "s_h1", "s_h1p", "s_h2", "s_hot", "s_w", "s_mid", "s_sum", "s_free", "s_dot", "s_dot3", "s_q1", "s_set"))
            s_rows = gathered2
            s_index, s_base = (sem(n, R) for n in ("s_index_e2", "s_base_e2"))
            with nc.Block() as block:
                @block.sync
                def _(sp):
                    sp.wait_ge(s_set, 1)
                    sp.dma_start(unit, a["vectors"]).then_inc(s_in, 16)
                    for i in range(2):
                        sp.dma_start(w0[i * NB:(i + 1) * NB, i * HID:(i + 1) * HID], a["L2_gnn_mlp_w0"]).then_inc(s_in, 16)
                        half = slice(i * HID, (i + 1) * HID)
                        sp.dma_start(w1[half, half], a["L2_gnn_mlp_w1"]).then_inc(s_in, 16)
                        sp.dma_start(w2[half, i, :], a["L2_gnn_mlp_w2"]).then_inc(s_in, 16)
                        sp.dma_start(b01[half, 0:1], a["L2_gnn_mlp_b0"].unsqueeze(1)).then_inc(s_in, 16)
                        sp.dma_start(b01[half, 1:2], a["L2_gnn_mlp_b1"].unsqueeze(1)).then_inc(s_in, 16)
                    sp.dma_start(b2[:, :], a["L2_gnn_mlp_b2"].unsqueeze(0).to_broadcast([3, P])).then_inc(s_in, 16)
                    sp.wait_ge(s_in, 16 * 12)
                    def load(n, g, r):
                        sp.wait_ge(s_mid, n + 1)
                        sp.dma_start(index[:, r, :], a["src_groups"][bass.ds(n, 1), :, :].rearrange("b p t -> (b p) t")).then_inc(s_index[r], 16)
                        sp.dma_start(base[:, r, :], basis.rearrange("g h i e -> (g h i) e")[bass.ds(n * 2 * NB, 2 * NB), :]).then_inc(s_base[r], 16)

                    ring(sp, EDGE_GROUPS, R, load)
                    for r in range(R):
                        sp.wait_ge(s_index[r], 16 * uses(EDGE_GROUPS, R, r))
                        sp.wait_ge(s_base[r], 16 * uses(EDGE_GROUPS, R, r))

                @block.gpsimd
                def _(pool):
                    def gather(n, g, r):
                        pool.wait_ge(s_index[r], 16 * g + 16)
                        pool.nop(nofuse=True)
                        for u in range(U):
                            nc.gpsimd.indirect_dma_start(
                                out=rows[:, r, u, :], out_offset=None, in_=table2[:, :],
                                in_offset=bass.IndirectOffsetOnAxis(ap=index[:, r, u:u + 1], axis=0)).then_inc(s_rows[r], 16)

                    ring(pool, EDGE_GROUPS, R, gather)
                    for r in range(R):
                        pool.wait_ge(s_rows[r], 16 * U * uses(EDGE_GROUPS, R, r))

                @block.scalar
                def _(act):
                    act.wait_ge(s_sq, 1)
                    nc.scalar.activation(length[:, :], square[:, :], ACT.Sqrt).then_inc(s_root, 1)

                    def silus(n, g, r):
                        act.wait_ge(s_h0, n + 1)
                        nc.scalar.activation(h1[:, :], psA[:, 0, :], ACT.Silu, bias=b01[:, 0:1]).then_inc(s_h1, 1)
                        act.wait_ge(s_h1p, n + 1)
                        nc.scalar.activation(h2[:, r % 2, :], psA[:, 1, :], ACT.Silu, bias=b01[:, 1:2]).then_inc(s_h2, 1)

                    ring(act, EDGE_GROUPS, R, silus)

                @block.vector
                def _(dve):
                    link = Chain(dve, s_chain)
                    link(nc.vector.memset(w0[:, :], 0.0))
                    link(nc.vector.memset(w1[:, :], 0.0))
                    link(nc.vector.memset(w2[:, :, :], 0.0))
                    dve.sem_inc(s_set, 1)
                    link(nc.vector.memset(ACC[:, :, :], 0.0))
                    link(nc.vector.memset(b2row[:, :], 0.0))
                    link(nc.vector.memset(three[:, :], 0.0))
                    dve.wait_ge(s_in, 16 * 12)
                    link(nc.vector.memset(three[0:3, :], 1.0))
                    link(nc.vector.tensor_copy(b2hi[:, :], b2[:, :]))
                    link(nc.vector.tensor_tensor(b2rest[:, :], b2[:, :], b2hi[:, :], ALU.subtract))
                    link(nc.vector.tensor_copy(b2mid[:, :], b2rest[:, :]))
                    link(nc.vector.tensor_tensor(b2rest[:, :], b2rest[:, :], b2mid[:, :], ALU.subtract))
                    link(nc.vector.tensor_copy(b2lo[:, :], b2rest[:, :]))
                    link(nc.vector.tensor_scalar(b2row[0:3, :], b2hi[:, :], K[0:3, 0:1], None, ALU.mult))
                    link(nc.vector.scalar_tensor_tensor(b2row[0:3, :], b2mid[:, :], K[0:3, 1:2], b2row[0:3, :], ALU.mult, ALU.add))
                    link(nc.vector.scalar_tensor_tensor(b2row[0:3, :], b2lo[:, :], K[0:3, 2:3], b2row[0:3, :], ALU.mult, ALU.add))
                    link(nc.vector.tensor_tensor(square[:, :], unit[:, :, 0], unit[:, :, 0], ALU.mult))
                    for c in range(1, 3):
                        link(nc.vector.tensor_tensor(length[:, :], unit[:, :, c], unit[:, :, c], ALU.mult))
                        link(nc.vector.tensor_tensor(square[:, :], square[:, :], length[:, :], ALU.add))
                    dve.sem_inc(s_sq, 1)
                    dve.wait_ge(s_root, 1)
                    link(nc.vector.tensor_scalar(length[:, :], length[:, :], 1e-12, None, ALU.add))
                    link(nc.vector.reciprocal(length[:, :], length[:, :]))
                    link(nc.vector.tensor_tensor(unit, unit, length[:, :].unsqueeze(2).to_broadcast([P, T, 3]), ALU.mult))
                    dve.sem_inc(s_mid, R)
                    dve.sem_inc(s_free, 4)

                    def add(n, firsts, u):
                        if firsts is not None:
                            dve.wait_ge(s_sum, n * U + (u + 1))
                            dve.wait_ge(s_free, n * U + (u + 4))
                            own = ACC[:, :, bass.ds(firsts[u], P)]
                            nc.vector.tensor_tensor(own, own, psS[:, u, :, 0:P], ALU.add).then_inc(s_free, 1)

                    def messages(n, g, r, before=None):
                        s = r % 2
                        one_hots(hot[:, s, :, :], n).then_inc(s_hot, 1)
                        dve.wait_ge(s_rows[r], 16 * U * g + 16 * U)
                        scalars = rows[:, r, :, 0:F]
                        vectors = rows[:, r, :, F:C].rearrange("p u (c k) -> p u c k", c=3)
                        along = unit[:, bass.ds(n * U, U), :].unsqueeze(3).to_broadcast([P, U, 3, F])
                        m1 = mid[:, s, :, 2 * F:5 * F].rearrange("p u (c k) -> p u c k", c=3)
                        m2 = mid[:, s, :, 5 * F:8 * F].rearrange("p u (c k) -> p u c k", c=3)
                        weights = [psW[:, s, :, i * F:(i + 1) * F] for i in range(4)]
                        dve.wait_ge(s_mid, n + R)
                        nc.vector.tensor_tensor(dot[:, :, :, :], vectors, along, ALU.mult).then_inc(s_dot, 1)
                        firsts = None if before is None else windows(dve, before * U)
                        dve.wait_ge(s_w, n + 1)
                        nc.vector.tensor_tensor(q1[:, :, :], weights[1], scalars, ALU.mult).then_inc(s_q1, 1)
                        add(before, firsts, 0)
                        dve.wait_ge(s_dot, 2 * n + 1)
                        nc.vector.tensor_tensor(dot[:, :, 0, :], dot[:, :, 0, :], dot[:, :, 1, :], ALU.add).then_inc(s_dot, 1)
                        dve.wait_ge(s_q1, n + 1)
                        nc.vector.tensor_tensor(m1, q1[:, :, :].unsqueeze(2).to_broadcast([P, U, 3, F]), along, ALU.mult)
                        add(before, firsts, 1)
                        dve.wait_ge(s_dot, 2 * n + 2)
                        nc.vector.tensor_tensor(dot[:, :, 1, :], dot[:, :, 0, :], dot[:, :, 2, :], ALU.add).then_inc(s_dot3, 1)
                        nc.vector.tensor_tensor(m2, weights[2].unsqueeze(2).to_broadcast([P, U, 3, F]), vectors, ALU.mult)
                        add(before, firsts, 2)
                        nc.vector.tensor_tensor(mid[:, s, :, 0:F], weights[0], scalars, ALU.mult)
                        dve.wait_ge(s_dot3, n + 1)
                        nc.vector.tensor_tensor(mid[:, s, :, F:2 * F], weights[3], dot[:, :, 1, :], ALU.mult).then_inc(s_mid, 1)
                        add(before, firsts, 3)

                    def step(n, g, r):
                        if isinstance(n, int) and n == last:
                            firsts = windows(dve, n * U)
                            for u in range(U):
                                add(n, firsts, u)
                        else:
                            messages(n + 1, g if r < R - 1 else g + 1, (r + 1) % R, n)

                    messages(0, 0, 0)
                    ring(dve, EDGE_GROUPS, R, step)

                @block.tensor
                def _(pe):
                    def radial(n, g, r, between=(lambda: None, lambda: None)):
                        pe.wait_ge(s_base[r], 16 * g + 16)
                        nc.tensor.matmul(psA[:, 0, :], w0[:, :], base[:, r, :], start=True, stop=True).then_inc(s_h0, 1)
                        between[0]()
                        pe.wait_ge(s_h1, n + 1)
                        nc.tensor.matmul(psA[:, 1, :], w1[:, :], h1[:, :], start=True, stop=True).then_inc(s_h1p, 1)
                        between[1]()
                        pe.wait_ge(s_h2, n + 1)
                        for u in range(U):
                            nc.tensor.matmul(psW[:, r % 2, u, :], h2[:, r % 2, (u % 2) * P:(u % 2 + 1) * P], w2[:, u // 2, :], start=True, stop=False)
                            done = nc.tensor.matmul(psW[:, r % 2, u, :], three[:, :], b2row[:, :], start=False, stop=True)
                        done.then_inc(s_w, 1)

                    def sums(n, r, tiles):
                        for u in tiles:
                            pe.wait_ge(s_free, n * U + (u + 1))
                            for b in range(2):
                                done = nc.tensor.matmul(psS[:, u, b, 0:P], mid[:, r % 2, u, b * C:(b + 1) * C], hot[:, r % 2, u, :], start=True, stop=True)
                            done.then_inc(s_sum, 1)

                    def step(n, g, r):
                        pe.wait_ge(s_hot, n + 1)
                        pe.wait_ge(s_mid, n + (R + 1))
                        if isinstance(n, int) and n + 2 > last:
                            sums(n, r, range(U))
                        else:
                            radial(n + 2, g if r < R - 2 else g + 1, (r + 2) % R,
                                   (lambda: sums(n, r, range(0, U // 2)), lambda: sums(n, r, range(U // 2, U))))

                    radial(0, 0, 0)
                    radial(1, 0, 1)
                    ring(pe, EDGE_GROUPS, R, step)

        def finish(L, load, n_load, prepare):
            with ExitStack() as st:
                sb, ps, sem = alloc(st)
                WA = sb(f"WA{L}", [P, 2, C])
                stage = sb(f"stage{L}", [P, TG * C])
                psP = ps(f"psP{L}", [P, 2, 512])
                psT = ps(f"psT_f{L}", [P, 8, C])
                s_in, s_ready, s_chain, s_proj, s_stage, s_turn, s_added = (sem(f"{n}_f{L}") for n in (
                    "s_in", "s_ready", "s_chain", "s_proj", "s_stage", "s_turn", "s_added"))
                with nc.Block() as block:
                    @block.sync
                    def _(sp):
                        load(sp, WA, s_in)
                        sp.wait_ge(s_in, 16 * n_load)

                    @block.vector
                    def _(dve):
                        link = Chain(dve, s_chain)
                        dve.wait_ge(s_in, 16 * n_load)
                        prepare(link, WA)
                        dve.sem_inc(s_ready, 1)
                        with dve.Fori(0, TN // TG) as g:
                            dve.wait_ge(s_turn, g + 1)
                            at = X[:, bass.ds(g * TG, TG), :]
                            nc.vector.tensor_tensor(at, at, psT[:, 0:TG, :], ALU.add).then_inc(s_added, 1)

                    @block.scalar
                    def _(act):
                        with act.Fori(0, TN // TG) as g:
                            act.wait_ge(s_proj, g + 1)
                            nc.scalar.copy(stage[:, :].rearrange("p (b e) -> p b e", b=2), psP[:, :, 0:TG * C // 2]).then_inc(s_stage, 1)

                    @block.tensor
                    def _(pe):
                        pe.wait_ge(s_ready, 1)
                        with pe.Fori(0, TN // TG) as g:
                            for b in range(2):
                                cols = bass.ds(g * (TG * C) + b * (TG * C // 2), TG * C // 2)
                                nc.tensor.matmul(psP[:, b, 0:TG * C // 2], WA[:, 0, :], ACC[:, 0, cols], start=True, stop=False)
                                last = nc.tensor.matmul(psP[:, b, 0:TG * C // 2], WA[:, 1, :], ACC[:, 1, cols], start=False, stop=True)
                            last.then_inc(s_proj, 1)
                            pe.wait_ge(s_stage, g + 1)
                            for i in range(TG):
                                last = nc.tensor.transpose(psT[:, i, :], stage[:, i * C:(i + 1) * C], ident)
                            last.then_inc(s_turn, 1)
                            pe.wait_ge(s_added, g + 1)

        with ExitStack() as st:
            sb, ps, sem = alloc(st)
            wst = sb("wst2", [P, 2, F])

            def load_out(sp, WA, s_in):
                sp.dma_start(wst[0:2 * F, 0, :], a["L2_gnn_W_out0"]).then_inc(s_in, 16)
                for part in range(2):
                    for c in range(3):
                        block, at = divmod(2 + 3 * part + c, 4)
                        sp.dma_start(wst[at * F:(at + 1) * F, block, :], a["L2_gnn_W_out1"][part * F:(part + 1) * F, :]).then_inc(s_in, 16)

            def prepare_out(link, WA):
                scale = 1.0 / ((2 * F) ** 0.5 * 16.0)
                link(nc.vector.memset(WA[:, :, :], 0.0))
                link(nc.vector.tensor_scalar(WA[0:2 * F, 0, 0:F], wst[0:2 * F, 0, :], scale, None, ALU.mult))
                for part in range(2):
                    for c in range(3):
                        block, at = divmod(2 + 3 * part + c, 4)
                        own = slice(at * F, (at + 1) * F)
                        link(nc.vector.tensor_scalar(WA[own, block, F + c:C:3], wst[own, block, :],
                                                     scale * (3.0 ** 0.5 if part == 0 else 1.0), None, ALU.mult))

            finish(2, load_out, 7, prepare_out)

        clear_semaphores()

        node_stage(3, C, table3, lambda sp, WT, WX, s_w: sp.dma_start(WT[:, :], a["L3_gnn_W"]).then_inc(s_w, 16), 1,
                   lambda link, WT, WX: None, scale=DINV)

        with ExitStack() as st:
            sb, ps, sem = alloc(st)
            R = 4
            last = EDGE_GROUPS - 1
            index = sb("index3", [P, R, U], I32)
            rows = sb("rows3", [P, R, U, C])
            hot = sb("hot3", [P, 2, U, P])
            psS = ps("psS3", [P, 4, 512])
            s_chain, s_hot, s_sum, s_free, s_done = (sem(n + "_e3") for n in ("s_chain", "s_hot", "s_sum", "s_free", "s_done"))
            s_rows = gathered3
            s_index = sem("s_index_e3", R)
            with nc.Block() as block:
                @block.sync
                def _(sp):
                    def load(n, g, r):
                        sp.wait_ge(s_done, n + 1)
                        sp.dma_start(index[:, r, :], a["src_groups"][bass.ds(n, 1), :, :].rearrange("b p t -> (b p) t")).then_inc(s_index[r], 16)

                    ring(sp, EDGE_GROUPS, R, load)
                    for r in range(R):
                        sp.wait_ge(s_index[r], 16 * uses(EDGE_GROUPS, R, r))

                @block.gpsimd
                def _(pool):
                    def gather(n, g, r):
                        pool.wait_ge(s_index[r], 16 * g + 16)
                        pool.nop(nofuse=True)
                        for u in range(U):
                            nc.gpsimd.indirect_dma_start(
                                out=rows[:, r, u, :], out_offset=None, in_=table3[:, :],
                                in_offset=bass.IndirectOffsetOnAxis(ap=index[:, r, u:u + 1], axis=0)).then_inc(s_rows[r], 16)

                    ring(pool, EDGE_GROUPS, R, gather)
                    for r in range(R):
                        pool.wait_ge(s_rows[r], 16 * U * uses(EDGE_GROUPS, R, r))

                @block.vector
                def _(dve):
                    link = Chain(dve, s_chain)
                    link(nc.vector.memset(ACC[:, 0, :], 0.0))
                    dve.sem_inc(s_done, R)
                    dve.sem_inc(s_free, 4)
                    one_hots(hot[:, 0, :, :], 0).then_inc(s_hot, 1)

                    def add(n, g, r):
                        if not (isinstance(n, int) and n == last):
                            one_hots(hot[:, (r + 1) % 2, :, :], n + 1).then_inc(s_hot, 1)
                        firsts = windows(dve, n * U)
                        for u in range(U):
                            dve.wait_ge(s_sum, n * U + (u + 1))
                            own = ACC[:, 0, bass.ds(firsts[u], P)]
                            nc.vector.tensor_tensor(own, own, psS[:, u, 0:P], ALU.add).then_inc(s_free, 1)
                            dve.wait_ge(s_free, n * U + (u + 5))
                        dve.sem_inc(s_done, 1)

                    ring(dve, EDGE_GROUPS, R, add)

                @block.tensor
                def _(pe):
                    def sums(n, g, r):
                        pe.wait_ge(s_hot, n + 1)
                        pe.wait_ge(s_rows[r], 16 * U * g + 16 * U)
                        for u in range(U):
                            pe.wait_ge(s_free, n * U + (u + 1))
                            nc.tensor.matmul(psS[:, u, 0:P], rows[:, r, u, :], hot[:, r % 2, u, :], start=True, stop=True).then_inc(s_sum, 1)

                    ring(pe, EDGE_GROUPS, R, sums)

        with ExitStack() as st:
            sb, ps, sem = alloc(st)
            own = sb("own3", [P, TN, C])
            AGG = ACC[:, 1, 0:TN * C].rearrange("p (t c) -> p t c", t=TN)
            hn = HN[:, 0:TN * C].rearrange("p (t c) -> p t c", t=TN)
            rowsB = sb("rowsB3", [P, 3, C])
            mean = sb("mean_f3", [P, TN])
            var = sb("var_f3", [P, TN])
            stage = sb("stage3", [P, TG * C])
            psT = ps("psT_f3", [P, 8, C])
            s_in, s_chain, s_stage, s_turn, s_added, s_var, s_sqrt = (sem(n + "_f3") for n in (
                "s_in", "s_chain", "s_stage", "s_turn", "s_added", "s_var", "s_sqrt"))
            with nc.Block() as block:
                @block.sync
                def _(sp):
                    sp.dma_start(own[:, :, :], table3[0:TN * P, :].rearrange("(t p) c -> p t c", p=P)).then_inc(s_in, 16)
                    for i, name in enumerate(("bias", "ln_gamma", "ln_beta")):
                        sp.dma_start(rowsB[:, i, :], a["L3_gnn_" + name].unsqueeze(0).to_broadcast([P, C])).then_inc(s_in, 16)
                    sp.wait_ge(s_in, 64)

                @block.scalar
                def _(act):
                    with act.Fori(0, TN // TG) as g:
                        nc.scalar.copy(stage[:, :], ACC[:, 0, bass.ds(g * TG * C, TG * C)]).then_inc(s_stage, 1)
                        act.wait_ge(s_turn, g + 1)
                    act.wait_ge(s_var, 1)
                    nc.scalar.activation(var[:, :], var[:, :], ACT.Sqrt).then_inc(s_sqrt, 1)

                @block.tensor
                def _(pe):
                    with pe.Fori(0, TN // TG) as g:
                        pe.wait_ge(s_stage, g + 1)
                        for i in range(TG):
                            done = nc.tensor.transpose(psT[:, i, :], stage[:, i * C:(i + 1) * C], ident)
                        done.then_inc(s_turn, 1)
                        pe.wait_ge(s_added, g + 1)

                @block.vector
                def _(dve):
                    link = Chain(dve, s_chain)
                    link(nc.vector.scalar_tensor_tensor(X[:, :, :], hn, 0.0, X[:, :, :], ALU.max, ALU.add))
                    dve.wait_ge(s_in, 64)
                    with dve.Fori(0, TN // TG) as g:
                        dve.wait_ge(s_turn, g + 1)
                        nc.vector.tensor_tensor(AGG[:, bass.ds(g * TG, TG), :], own[:, bass.ds(g * TG, TG), :], psT[:, 0:TG, :], ALU.add).then_inc(s_added, 1)
                    dve.wait_ge(s_added, TN // TG)

                    def per_node(v):
                        return v.unsqueeze(2).to_broadcast([P, TN, C])

                    def per_channel(i):
                        return rowsB[:, i, :].unsqueeze(1).to_broadcast([P, TN, C])

                    link(nc.vector.tensor_tensor(AGG, AGG, per_node(DINV[:, :]), ALU.mult))
                    link(nc.vector.tensor_tensor(AGG, AGG, per_channel(0), ALU.add))
                    link(nc.vector.reduce_sum(mean[:, :], AGG, axis=AX))
                    link(nc.vector.tensor_scalar(mean[:, :], mean[:, :], 1.0 / C, None, ALU.mult))
                    link(nc.vector.tensor_tensor(AGG, AGG, per_node(mean[:, :]), ALU.subtract))
                    link(nc.vector.tensor_tensor(own[:, :, :], AGG, AGG, ALU.mult))
                    link(nc.vector.reduce_sum(var[:, :], own[:, :, :], axis=AX))
                    nc.vector.tensor_scalar(var[:, :], var[:, :], 1.0 / C, EPS, ALU.mult, ALU.add).then_inc(s_var, 1)
                    dve.wait_ge(s_sqrt, 1)
                    link(nc.vector.reciprocal(var[:, :], var[:, :]))
                    link(nc.vector.tensor_tensor(AGG, AGG, per_node(var[:, :]), ALU.mult))
                    link(nc.vector.tensor_tensor(AGG, AGG, per_channel(1), ALU.mult))
                    link(nc.vector.tensor_tensor(AGG, AGG, per_channel(2), ALU.add))
                    link(nc.vector.tensor_scalar(AGG, AGG, 0.0, None, ALU.max))
                    link(nc.vector.tensor_tensor(X[:, :, :], X[:, :, :], AGG, ALU.add))

        with ExitStack() as st:
            _, _, sem = alloc(st)
            s_res = sem("s_res")
            with nc.Block() as block:
                @block.sync
                def _(sp):
                    sp.dma_start(out[0:(TN - 1) * P, :].rearrange("(t p) c -> p t c", p=P), X[:, 0:TN - 1, :]).then_inc(s_res, 16)
                    sp.dma_start(out[(TN - 1) * P:N, :], X[0:N - (TN - 1) * P, TN - 1, :]).then_inc(s_res, 16)
                    sp.wait_ge(s_res, 32)


_OUT = ((N, C), "float32")


def kernel(**inputs):
    import concourse.bacc as bacc
    from concourse.bass_utils import run_bass_kernel_spmd as run

    nc = bacc.Bacc("TRN2", target_bir_lowering=False, num_devices=1)
    pad = T * P - E
    src = np.pad(np.asarray(inputs["src"]), (0, pad)).reshape(T, P)
    dst = np.pad(np.asarray(inputs["dst"]), (0, pad), constant_values=N).reshape(T, P)
    weight = np.pad(np.asarray(inputs["edge_weight"]), (0, pad)).reshape(T, P)
    vectors = np.pad(np.asarray(inputs["edge_attr_3"]), ((0, pad), (0, 0)), constant_values=1.0).reshape(T, P, 3)
    arrays = {
        "consts": constants(), "x": inputs["x"],
        "src_rows": src, "dst_rows": dst, "weight_rows": weight,
        "src_cols": src.T, "dst_cols": dst.T, "weight_cols": weight.T,
        "dst_first": dst[None, :, 0], "dst_last": dst[None, :, P - 1],
        "src_groups": src.reshape(T // U, U, P).transpose(0, 2, 1),
        "src_batches": src.reshape(T // B0, B0, P).transpose(0, 2, 1),
        "vectors": vectors.transpose(1, 0, 2),
        "L1_gnn_lin1_w": np.asarray(inputs["L1_gnn_lin1_w"]).T, "L1_gnn_lin2_w": np.asarray(inputs["L1_gnn_lin2_w"]).T,
    }
    for name in inputs:
        if name.startswith("L") and name not in arrays:
            arrays[name] = inputs[name]
    arrays = {"in_" + k: np.ascontiguousarray(v) for k, v in arrays.items()}
    a = {k[3:]: nc.dram_tensor(k, v.shape, mybir.dt.from_np(v.dtype), kind="ExternalInput").ap() for k, v in arrays.items()}
    out = nc.dram_tensor("out", _OUT[0], F32, kind="ExternalOutput").ap()
    build(nc, a, out)
    r = run(nc, [arrays], core_ids=[0])
    return r.results[0]["out"]
```
